# Optimizing a Trainium2 kernel written in Bass

```python
import numpy as np
import jax
import jax.numpy as jnp

def _softmax(x, axis=-1):
    return jax.nn.softmax(x, axis=axis)

def _gelu(x):
    return jax.nn.gelu(x, approximate=True)

def _silu(x):
    return jax.nn.silu(x)

def _sigmoid(x):
    return jax.nn.sigmoid(x)

def _layernorm(x, axis=-1, eps=1e-05):
    m = jnp.mean(x, axis=axis, keepdims=True)
    v = jnp.var(x, axis=axis, keepdims=True)
    return (x - m) / jnp.sqrt(v + eps)

def _scatter_add(tgt, idx, src, axis=0):
    return tgt.at[idx].add(src)

def _segment_sum(src, seg, n):
    return jax.ops.segment_sum(src, seg, n)
kernel_name = 'mk_seq_preln_d1_jaxref_r8_916aeb'

def setup_inputs(seed: int=0):
    np.random.seed(seed)
    _w = jnp.asarray

    def _L0_attn_setup():
        import jax, jax.numpy as jnp
        import numpy as np
        import math
        DIM = 128
        NUM_HEADS = 16
        HEAD_DIM = DIM // NUM_HEADS
        BATCH = 4
        SEQ = 512

        def _feature_map(x, R):
            x = x / math.sqrt(HEAD_DIM)
            proj = jnp.einsum('bhnd,dm->bhnm', x, R)
            sq_norm = jnp.sum(x * x, axis=-1, keepdims=True)
            return jnp.exp(proj - 0.5 * sq_norm)
        key = jax.random.key(seed)
        ks = jax.random.split(key, 10)
        s = 1.0 / math.sqrt(DIM)
        return {'x': jax.random.normal(ks[0], (BATCH, SEQ, DIM), dtype=jnp.float32), 'Wq': jax.random.normal(ks[1], (DIM, DIM), dtype=jnp.float32) * s, 'bq': jax.random.normal(ks[2], (DIM,), dtype=jnp.float32) * 0.01, 'Wk': jax.random.normal(ks[3], (DIM, DIM), dtype=jnp.float32) * s, 'bk': jax.random.normal(ks[4], (DIM,), dtype=jnp.float32) * 0.01, 'Wv': jax.random.normal(ks[5], (DIM, DIM), dtype=jnp.float32) * s, 'bv': jax.random.normal(ks[6], (DIM,), dtype=jnp.float32) * 0.01, 'Wo': jax.random.normal(ks[7], (DIM, DIM), dtype=jnp.float32) * s, 'bo': jax.random.normal(ks[8], (DIM,), dtype=jnp.float32) * 0.01, 'R': jax.random.normal(ks[9], (HEAD_DIM, HEAD_DIM), dtype=jnp.float32) * 0.4}
    _L0_attn_in = _L0_attn_setup()

    def _L0_ffn_setup():
        import jax, jax.numpy as jnp
        import numpy as np
        B, L, D = (4, 256, 128)
        H = 16
        E = 16
        NS = 16
        S = NS // E
        F = 512
        EPS = 1e-05

        def _layernorm(x, g, b):
            mu = jnp.mean(x, axis=-1, keepdims=True)
            var = jnp.mean(jnp.square(x - mu), axis=-1, keepdims=True)
            return (x - mu) * jax.lax.rsqrt(var + EPS) * g + b

        def _mha(q, k, v, Wq, bq, Wk, bk, Wv, bv, Wo, bo):
            Bq, Lq, Dm = q.shape
            dh = Dm // H
            qh = (q @ Wq + bq).reshape(Bq, Lq, H, dh)
            kh = (k @ Wk + bk).reshape(Bq, -1, H, dh)
            vh = (v @ Wv + bv).reshape(Bq, -1, H, dh)
            scores = jnp.einsum('bqhd,bkhd->bhqk', qh, kh) / jnp.asarray(np.sqrt(dh), q.dtype)
            attn = jax.nn.softmax(scores, axis=-1)
            out = jnp.einsum('bhqk,bkhd->bqhd', attn, vh).reshape(Bq, Lq, Dm)
            return out @ Wo + bo
        key = jax.random.key(seed)
        ks = jax.random.split(key, 32)
        s = 0.02
        d = {}
        d['x'] = jax.random.normal(ks[0], (B, L, D), jnp.float32)
        d['slot_query'] = jax.random.normal(ks[1], (1, NS, D), jnp.float32) * 0.01
        for i, nm in enumerate(['d_Wq', 'd_Wk', 'd_Wv', 'd_Wo']):
            d[nm] = jax.random.normal(ks[2 + i], (D, D), jnp.float32) * s
        for nm in ['d_bq', 'd_bk', 'd_bv', 'd_bo']:
            d[nm] = jnp.zeros((D,), jnp.float32)
        for i, nm in enumerate(['c_Wq', 'c_Wk', 'c_Wv', 'c_Wo']):
            d[nm] = jax.random.normal(ks[6 + i], (D, D), jnp.float32) * s
        for nm in ['c_bq', 'c_bk', 'c_bv', 'c_bo']:
            d[nm] = jnp.zeros((D,), jnp.float32)
        d['e_ln_g'] = jnp.ones((E, D), jnp.float32)
        d['e_ln_b'] = jnp.zeros((E, D), jnp.float32)
        d['e_W1'] = jax.random.normal(ks[10], (E, D, F), jnp.float32) * s
        d['e_b1'] = jnp.zeros((E, F), jnp.float32)
        d['e_Wg'] = jax.random.normal(ks[11], (E, D, F), jnp.float32) * s
        d['e_bg'] = jnp.zeros((E, F), jnp.float32)
        d['e_W2'] = jax.random.normal(ks[12], (E, F, D), jnp.float32) * s
        d['e_b2'] = jnp.zeros((E, D), jnp.float32)
        return d
    _L0_ffn_in = _L0_ffn_setup()
    _d = {'L0_attn_x': _L0_attn_in['x'], 'L0_attn_Wq': _L0_attn_in['Wq'], 'L0_attn_bq': _L0_attn_in['bq'], 'L0_attn_Wk': _L0_attn_in['Wk'], 'L0_attn_bk': _L0_attn_in['bk'], 'L0_attn_Wv': _L0_attn_in['Wv'], 'L0_attn_bv': _L0_attn_in['bv'], 'L0_attn_Wo': _L0_attn_in['Wo'], 'L0_attn_bo': _L0_attn_in['bo'], 'L0_attn_R': _L0_attn_in['R'], 'L0_ffn_slot_query': _L0_ffn_in['slot_query'], 'L0_ffn_d_Wq': _L0_ffn_in['d_Wq'], 'L0_ffn_d_Wk': _L0_ffn_in['d_Wk'], 'L0_ffn_d_Wv': _L0_ffn_in['d_Wv'], 'L0_ffn_d_Wo': _L0_ffn_in['d_Wo'], 'L0_ffn_d_bq': _L0_ffn_in['d_bq'], 'L0_ffn_d_bk': _L0_ffn_in['d_bk'], 'L0_ffn_d_bv': _L0_ffn_in['d_bv'], 'L0_ffn_d_bo': _L0_ffn_in['d_bo'], 'L0_ffn_c_Wq': _L0_ffn_in['c_Wq'], 'L0_ffn_c_Wk': _L0_ffn_in['c_Wk'], 'L0_ffn_c_Wv': _L0_ffn_in['c_Wv'], 'L0_ffn_c_Wo': _L0_ffn_in['c_Wo'], 'L0_ffn_c_bq': _L0_ffn_in['c_bq'], 'L0_ffn_c_bk': _L0_ffn_in['c_bk'], 'L0_ffn_c_bv': _L0_ffn_in['c_bv'], 'L0_ffn_c_bo': _L0_ffn_in['c_bo'], 'L0_ffn_e_ln_g': _L0_ffn_in['e_ln_g'], 'L0_ffn_e_ln_b': _L0_ffn_in['e_ln_b'], 'L0_ffn_e_W1': _L0_ffn_in['e_W1'], 'L0_ffn_e_b1': _L0_ffn_in['e_b1'], 'L0_ffn_e_Wg': _L0_ffn_in['e_Wg'], 'L0_ffn_e_bg': _L0_ffn_in['e_bg'], 'L0_ffn_e_W2': _L0_ffn_in['e_W2'], 'L0_ffn_e_b2': _L0_ffn_in['e_b2']}
    _x0 = _d['L0_attn_x']
    _d['L0_attn_x'] = jax.random.normal(jax.random.fold_in(jax.random.key(seed), 1), (16, 256, 128), dtype=_x0.dtype)
    del _x0
    return _d

def reference(L0_attn_x, L0_attn_Wq, L0_attn_bq, L0_attn_Wk, L0_attn_bk, L0_attn_Wv, L0_attn_bv, L0_attn_Wo, L0_attn_bo, L0_attn_R, L0_ffn_slot_query, L0_ffn_d_Wq, L0_ffn_d_Wk, L0_ffn_d_Wv, L0_ffn_d_Wo, L0_ffn_d_bq, L0_ffn_d_bk, L0_ffn_d_bv, L0_ffn_d_bo, L0_ffn_c_Wq, L0_ffn_c_Wk, L0_ffn_c_Wv, L0_ffn_c_Wo, L0_ffn_c_bq, L0_ffn_c_bk, L0_ffn_c_bv, L0_ffn_c_bo, L0_ffn_e_ln_g, L0_ffn_e_ln_b, L0_ffn_e_W1, L0_ffn_e_b1, L0_ffn_e_Wg, L0_ffn_e_bg, L0_ffn_e_W2, L0_ffn_e_b2):

    def _L0_attn_ref(x, Wq, bq, Wk, bk, Wv, bv, Wo, bo, R):
        import jax, jax.numpy as jnp
        import numpy as np
        import math
        DIM = 128
        NUM_HEADS = 16
        HEAD_DIM = DIM // NUM_HEADS
        BATCH = 4
        SEQ = 512

        def _feature_map(x, R):
            x = x / math.sqrt(HEAD_DIM)
            proj = jnp.einsum('bhnd,dm->bhnm', x, R)
            sq_norm = jnp.sum(x * x, axis=-1, keepdims=True)
            return jnp.exp(proj - 0.5 * sq_norm)
        b, n, _ = x.shape
        h, d = (NUM_HEADS, HEAD_DIM)

        def split_heads(t):
            return t.reshape(b, n, h, d).transpose(0, 2, 1, 3)
        q = split_heads(x @ Wq.T + bq)
        k = split_heads(x @ Wk.T + bk)
        v = split_heads(x @ Wv.T + bv)
        q_prime = _feature_map(q, R)
        k_prime = _feature_map(k, R)
        kv = jnp.einsum('bhnd,bhne->bhde', k_prime, v)
        z = 1.0 / (jnp.sum(q_prime, axis=-1) + 1e-08)
        out = jnp.einsum('bhnd,bhde,bhn->bhne', q_prime, kv, z)
        out = out.transpose(0, 2, 1, 3).reshape(b, n, DIM)
        return out @ Wo.T + bo

    def _L0_ffn_ref(x, slot_query, d_Wq, d_Wk, d_Wv, d_Wo, d_bq, d_bk, d_bv, d_bo, c_Wq, c_Wk, c_Wv, c_Wo, c_bq, c_bk, c_bv, c_bo, e_ln_g, e_ln_b, e_W1, e_b1, e_Wg, e_bg, e_W2, e_b2):
        import jax, jax.numpy as jnp
        import numpy as np
        B, L, D = (4, 256, 128)
        H = 16
        E = 16
        NS = 16
        S = NS // E
        F = 512
        EPS = 1e-05

        def _layernorm(x, g, b):
            mu = jnp.mean(x, axis=-1, keepdims=True)
            var = jnp.mean(jnp.square(x - mu), axis=-1, keepdims=True)
            return (x - mu) * jax.lax.rsqrt(var + EPS) * g + b

        def _mha(q, k, v, Wq, bq, Wk, bk, Wv, bv, Wo, bo):
            Bq, Lq, Dm = q.shape
            dh = Dm // H
            qh = (q @ Wq + bq).reshape(Bq, Lq, H, dh)
            kh = (k @ Wk + bk).reshape(Bq, -1, H, dh)
            vh = (v @ Wv + bv).reshape(Bq, -1, H, dh)
            scores = jnp.einsum('bqhd,bkhd->bhqk', qh, kh) / jnp.asarray(np.sqrt(dh), q.dtype)
            attn = jax.nn.softmax(scores, axis=-1)
            out = jnp.einsum('bhqk,bkhd->bqhd', attn, vh).reshape(Bq, Lq, Dm)
            return out @ Wo + bo
        Bx = x.shape[0]
        q = jnp.broadcast_to(slot_query, (Bx, NS, D))
        o = q + _mha(q, x, x, d_Wq, d_bq, d_Wk, d_bk, d_Wv, d_bv, d_Wo, d_bo)
        os = o.reshape(Bx, E, S, D)
        h = _layernorm(os, e_ln_g[None, :, None, :], e_ln_b[None, :, None, :])
        u = jax.nn.silu(jnp.einsum('besd,edf->besf', h, e_W1) + e_b1[None, :, None, :])
        g = jax.nn.silu(jnp.einsum('besd,edf->besf', h, e_Wg) + e_bg[None, :, None, :])
        y = jnp.einsum('besf,efd->besd', u * g, e_W2) + e_b2[None, :, None, :]
        o = o + y.reshape(Bx, NS, D)
        out = _mha(x, o, o, c_Wq, c_bq, c_Wk, c_bk, c_Wv, c_bv, c_Wo, c_bo)
        return out
    x = L0_attn_x
    x = x + _L0_attn_ref(_layernorm(x, axis=-1), L0_attn_Wq, L0_attn_bq, L0_attn_Wk, L0_attn_bk, L0_attn_Wv, L0_attn_bv, L0_attn_Wo, L0_attn_bo, L0_attn_R)
    x = x + _L0_ffn_ref(_layernorm(x, axis=-1), L0_ffn_slot_query, L0_ffn_d_Wq, L0_ffn_d_Wk, L0_ffn_d_Wv, L0_ffn_d_Wo, L0_ffn_d_bq, L0_ffn_d_bk, L0_ffn_d_bv, L0_ffn_d_bo, L0_ffn_c_Wq, L0_ffn_c_Wk, L0_ffn_c_Wv, L0_ffn_c_Wo, L0_ffn_c_bq, L0_ffn_c_bk, L0_ffn_c_bv, L0_ffn_c_bo, L0_ffn_e_ln_g, L0_ffn_e_ln_b, L0_ffn_e_W1, L0_ffn_e_b1, L0_ffn_e_Wg, L0_ffn_e_bg, L0_ffn_e_W2, L0_ffn_e_b2)
    return x

_drawn_inputs = setup_inputs


def setup_inputs(seed=0):
    import zlib

    import numpy as np

    out = dict(_drawn_inputs(seed))
    spreads = {'L0_ffn_d_bq': (0.0, 0.8),
     'L0_ffn_d_bk': (0.0, 2.0),
     'L0_ffn_d_bv': (0.0, 0.8),
     'L0_ffn_d_bo': (0.0, 0.8),
     'L0_ffn_c_bq': (0.0, 0.8),
     'L0_ffn_c_bk': (0.0, 2.0),
     'L0_ffn_c_bv': (0.0, 2.0),
     'L0_ffn_c_bo': (0.0, 2.0),
     'L0_ffn_e_ln_g': (1.0, 0.6),
     'L0_ffn_e_ln_b': (0.0, 0.8),
     'L0_ffn_e_b1': (0.0, 0.8),
     'L0_ffn_e_bg': (0.0, 0.8),
     'L0_ffn_e_b2': (0.0, 0.8)}
    factors = {'L0_attn_bq': 8.0,
     'L0_attn_bk': 8.0,
     'L0_attn_bo': 8.0,
     'L0_ffn_slot_query': 8.0,
     'L0_ffn_d_Wq': 32.861,
     'L0_ffn_d_Wk': 8.0,
     'L0_ffn_d_Wv': 8.0,
     'L0_ffn_d_Wo': 8.0,
     'L0_ffn_c_Wq': 8.0,
     'L0_ffn_c_Wk': 8.0,
     'L0_ffn_c_Wv': 8.0,
     'L0_ffn_c_Wo': 8.0,
     'L0_ffn_e_W1': 8.0,
     'L0_ffn_e_Wg': 8.0,
     'L0_ffn_e_W2': 8.0}
    for name, (base, spread) in spreads.items():
        noise = np.random.default_rng([zlib.crc32(name.encode()), seed]).standard_normal(out[name].shape)
        drawn = base * np.exp(spread * noise) if base else spread * noise
        out[name] = jnp.asarray(drawn.astype(out[name].dtype))
    for name, factor in factors.items():
        out[name] = (out[name] * factor).astype(out[name].dtype)
    return out
```

```python
from contextlib import ExitStack

import numpy as np
import concourse.bass as bass
from concourse import mybir

F32 = mybir.dt.float32
ACT = mybir.ActivationFunctionType
ALU = mybir.AluOpType
AX = mybir.AxisListType

P = 128
NB = 16
NT = 256
H = 16
DH = P // H
S = 16
HS = H * S
FC = 4
EG = 4
L = P - 1
EPS = 1e-5
SC = float(1.0 / np.sqrt(DH))

AQ, AK, AV, AO, DK, DV, CQ, DQ, DO, CK, CV, CO = range(12)
SLOT, GAIN, SHIFT, B2, BIAS = 0, 16, 32, 48, 64
BQ, BK, BV, BDK, BDV, BCQ, BDQ, BCK, BCV = range(BIAS, BIAS + 9)
NR = BIAS + 9


def turn(half, par, lag):
    return half * 2 + (par - lag), (par - lag) % 2, half + (par - lag) // 2


def live(half, par, lag):
    return not isinstance(half, int) or 0 <= 2 * half + par - lag < NB


def wait(eng, sem, n, most=NB):
    if isinstance(n, int):
        n = min(n, most)
        if n <= 0:
            return
    eng.wait_ge(sem, n)


def pipeline(eng, step, steps, first, last):
    for t in range(first):
        step(t // 2, t % 2)
    with eng.Fori(0, (last - first) // 2) as i:
        step(i + first // 2, 0)
        step(i + first // 2, 1)
    for t in range(last, steps):
        step(t // 2, t % 2)


LAGS1, FIRST1 = 7, 8
LAGS2, FIRST2 = 5, 6


def build(nc, x, a_Wq, a_bq, a_Wk, a_bk, a_Wv, a_bv, a_Wo, a_bo, R, slot, d_Wq, d_Wk, d_Wv, d_Wo,
          d_bq, d_bk, d_bv, d_bo, c_Wq, c_Wk, c_Wv, c_Wo, c_bq, c_bk, c_bv, c_bo, ln_g, ln_b,
          W1, b1, Wg, bg, W2, b2, out):
    ctx = ExitStack()
    with ctx:
        def sb(name, *shape):
            return ctx.enter_context(nc.sbuf_tensor(name, list(shape), F32))

        def sem(name):
            return ctx.enter_context(nc.semaphore(name))

        X = sb("X", P, NB, NT)
        XN2T = sb("XN2T", P, NB, NT)
        W = sb("W", P, 12, P)
        W1s = sb("W1s", P, S, FC * P)
        Wgs = sb("Wgs", P, S, FC * P)
        W2s = sb("W2s", P, S, FC, P)
        vec = sb("vec", NR, P)
        vecT = sb("vecT", P, NR)
        fvec = sb("fvec", P, P)
        fvecT = sb("fvecT", P, 2, S * FC)
        a_bo_all = sb("a_bo_all", P, P)
        c_bo_all = sb("c_bo_all", P, P)
        d_bo_all = sb("d_bo_all", S, P)
        Rrep = sb("Rrep", P, DH)
        ident = sb("ident", P, P)
        head8 = sb("head8", P, H)
        head16 = sb("head16", P, P // S)
        sel3 = sb("sel3", P, P // S, S)
        selS = sb("selS", P, S)
        repS = sb("repS", S, S, NB)
        epsT = sb("epsT", P, 2)
        mhalf = sb("mhalf", P, 2)
        Wt = sb("Wt", P, 3, P)
        Wproj = sb("Wproj", P, 4 * P)
        WvP = sb("WvP", P, P)
        WoT = sb("WoT", P, P)
        BDR = sb("BDR", P, P)
        dWvP = sb("dWvP", P, P)
        qTs = sb("qTs", P, S)
        qbd = sb("qbd", P, HS)
        Ad = sb("Ad", P, HS)
        slotb = sb("slotb", S, P)
        st1 = sb("st1", P, 2, 2, 6)
        mv1 = sb("mv1", P, 2, 2, 2)
        ve1 = sb("ve1", P, 2, 2)
        rs1 = sb("rs1", P, 2, 2)
        xn = sb("xn", P, 2, 2, P)
        xnT = sb("xnT", P, 2, NT)
        sq = sb("sq", P, 2, 2, 2 * P)
        ss = sb("ss", P, 2, 4 * H)
        ex = sb("ex", P, 2, 2, 2 * P)
        ft = sb("ft", P, 2, 2, 2 * P)
        Vs = sb("Vs", P, 2, 2, P)
        den = sb("den", P, 2, 2 * H)
        den2 = sb("den2", P, 2, 2 * H)
        rz = sb("rz", P, 2, 2 * H)
        qz = sb("qz", P, 2, 2, P)
        qzT = sb("qzT", P, 2, NT)
        kvm = sb("kvm", P, 2, P)
        Mb = sb("Mb", P, 2, P)
        st2 = sb("st2", P, 2, 2, 6)
        mv2 = sb("mv2", P, 2, 2, 2)
        ve2 = sb("ve2", P, 2, 2)
        rs2 = sb("rs2", P, 2, 2)
        xn2 = sb("xn2", P, 2, 2, P)
        xn2T = sb("xn2T", P, 2, NT)
        nmax = sb("nmax", P, 2, 2)
        pr = sb("pr", P, 2, 2, NT)
        psm = sb("psm", P, 2, 2)
        rps = sb("rps", P, 2, 2)
        prT = sb("prT", P, 2, 2, HS)
        V2s = sb("V2s", P, 2, 2, P)
        pvm = sb("pvm", P, 2, 2, P)
        aoT = sb("aoT", P, S, NB)
        o1 = sb("o1", P, 2, P)
        st3 = sb("st3", P, 2, 6)
        mv3 = sb("mv3", P, 2, 2)
        ve3 = sb("ve3", P, 2)
        rs3 = sb("rs3", P, 2)
        xh = sb("xh", P, 2, P)
        o1b = sb("o1b", P, S, NB)
        hg = sb("hg", P, S, NB)
        hT = sb("hT", P, S, NB)
        ug, th, sg = ex, ft, pr
        act = sb("act", P, 2, EG, FC, NB)
        o2T = sb("o2T", P, S * NB)
        kT = sb("kT", P, S, NB)
        vT = sb("vT", P, S, NB)
        xs = xn2T
        BDk = xnT
        BDv = qzT
        flat = "p k j m -> p k (j m)"
        As = sq[:, :, 0, :]
        VWs = sq[:, :, 1, :]
        sx = ex[:, :, :, :].rearrange(flat)
        ep = ft[:, :, :, :].rearrange(flat)
        at = pr[:, :, :, :].rearrange(flat)
        atT = prT
        mx = sb("mx", P, 2, 2 * H)
        sm = sb("sm", P, 2, 2 * H)
        rsm = sb("rsm", P, 2, 2 * H)
        ob = V2s[:, :, :, :].rearrange(flat)

        ps = ctx.enter_context(nc.psum_tensor("ps", [P, 8, 512], F32))

        x_in = [sem(f"x_in{g}") for g in range(4)]
        w_in, e_in = sem("w_in"), sem("e_in")
        pool_own, ident_ok, masks_ok = sem("pool_own"), sem("ident_ok"), sem("masks_ok")
        su_pe, su_act, su_dve = sem("su_pe"), sem("su_act"), sem("su_dve")
        bn1_ok, mv1_ok, ve1_ok, rs1_ok, xn_ok = (sem(n) for n in ("bn1_ok", "mv1_ok", "ve1_ok", "rs1_ok", "xn_ok"))
        xbo_ok = sem("xbo_ok")
        tx_ok, xnT_ok, proj_ok, vp_ok, v_ok = (sem(n) for n in ("tx_ok", "xnT_ok", "proj_ok", "vp_ok", "v_ok"))
        sq_ok, ss_ok, ex_ok, ft_ok = (sem(n) for n in ("sq_ok", "ss_ok", "ex_ok", "ft_ok"))
        den_ok, den2_ok, rz_ok, qz_ok = (sem(n) for n in ("den_ok", "den2_ok", "rz_ok", "qz_ok"))
        kv_ok, kvm_ok, mp_ok, mb_ok = (sem(n) for n in ("kv_ok", "kvm_ok", "mp_ok", "mb_ok"))
        tq_ok, qzT_ok, out_ok, x2_ok = (sem(n) for n in ("tq_ok", "qzT_ok", "out_ok", "x2_ok"))
        bn2_ok, mv2_ok, ve2_ok, rs2_ok, xn2_ok = (sem(n) for n in ("bn2_ok", "mv2_ok", "ve2_ok", "rs2_ok", "xn2_ok"))
        tx2_ok, xn2T_ok, s_ok, nmax_ok = (sem(n) for n in ("tx2_ok", "xn2T_ok", "s_ok", "nmax_ok"))
        v2p_ok, v2_ok, pr_ok, tp_ok, prT_ok = (sem(n) for n in ("v2p_ok", "v2_ok", "pr_ok", "tp_ok", "prT_ok"))
        pv_ok, rps_ok, pvm_ok, sel_ok, ao_ok = (sem(n) for n in ("pv_ok", "rps_ok", "pvm_ok", "sel_ok", "ao_ok"))
        xcbo_ok = sem("xcbo_ok")
        passed, dve_carry, sp_carry = sem("passed"), sem("dve_carry"), sem("sp_carry")
        mid_pe, mid_act, mid_dve, mid_pool = sem("mid_pe"), sem("mid_act"), sem("mid_dve"), sem("mid_pool")
        up_ok, ug_ok, th_ok, sg_ok, act_ok, y_ok = (sem(n) for n in ("up_ok", "ug_ok", "th_ok", "sg_ok", "act_ok", "y_ok"))
        o2_ok, kvp_ok, kT_ok, vT_ok = (sem(n) for n in ("o2_ok", "kvp_ok", "kT_ok", "vT_ok"))
        saved = [sem("saved0"), sem("saved1")]
        xs_in = [sem("xs_in0"), sem("xs_in1")]
        stored = [sem("stored0"), sem("stored1")]
        bdk_ok, bdv_ok, ap_ok, a_ok = (sem(n) for n in ("bdk_ok", "bdv_ok", "ap_ok", "a_ok"))
        vwp_ok, vw_ok = sem("vwp_ok"), sem("vw_ok")
        sp_ok, mx_ok, sx_ok, ep_ok = (sem(n) for n in ("sp_ok", "mx_ok", "sx_ok", "ep_ok"))
        sm_ok, rsm_ok, at_ok, tt_ok, atT_ok = (sem(n) for n in ("sm_ok", "rsm_ok", "at_ok", "tt_ok", "atT_ok"))
        op_ok, ob_ok = sem("op_ok"), sem("ob_ok")

        x_rows = x.rearrange("b (p j) d -> p b (j d)", j=2)
        out_rows = out.rearrange("b (p j) d -> p b (j d)", j=2)

        def over(ap, n):
            return ap.unsqueeze(2).broadcast_to([ap.shape[0], ap.shape[1], n])

        def under(ap, n):
            return ap.unsqueeze(1).broadcast_to([ap.shape[0], n, ap.shape[1]])

        def heads(ap, n):
            return ap.rearrange("p (m n) -> p m n", n=n)

        block = ctx.enter_context(nc.Block())

        N_SMALL = 12 + 4 + 9 + 2 + 4

        @block.sync
        def _(sp):
            for m, w in enumerate((a_Wq, a_Wk, a_Wv, a_Wo, d_Wk, d_Wv, c_Wq, d_Wq, d_Wo, c_Wk, c_Wv, c_Wo)):
                sp.dma_start(W[:, m, :], w).then_inc(w_in, 16)
            for r, t in ((SLOT, slot.rearrange("o s d -> (o s) d")), (GAIN, ln_g), (SHIFT, ln_b), (B2, b2)):
                sp.dma_start(vec[r:r + S, :], t).then_inc(w_in, 16)
            for r, t in ((BQ, a_bq), (BK, a_bk), (BV, a_bv), (BDK, d_bk), (BDV, d_bv), (BCQ, c_bq),
                         (BDQ, d_bq), (BCK, c_bk), (BCV, c_bv)):
                sp.dma_start(vec[r:r + 1, :], t.rearrange("(o d) -> o d", o=1)).then_inc(w_in, 16)
            for r, t in ((0, b1), (S * FC, bg)):
                sp.dma_start(fvec[r:r + S * FC, :], t.rearrange("e (c f) -> (e c) f", c=FC)).then_inc(w_in, 16)
            sp.dma_start(a_bo_all[:, :], a_bo.partition_broadcast(P)).then_inc(w_in, 16)
            sp.dma_start(c_bo_all[:, :], c_bo.partition_broadcast(P)).then_inc(w_in, 16)
            sp.dma_start(d_bo_all[:, :], d_bo.partition_broadcast(S)).then_inc(w_in, 16)
            sp.dma_start(Rrep[:, :], R.unsqueeze(0).broadcast_to([H, DH, DH])).then_inc(w_in, 16)
            for g in range(0, S, 4):
                sp.dma_start(W1s[:, g:g + 4, :], W1[g:g + 4].rearrange("e d f -> d e f")).then_inc(e_in, 16)
                sp.dma_start(Wgs[:, g:g + 4, :], Wg[g:g + 4].rearrange("e d f -> d e f")).then_inc(e_in, 16)
                for e in range(g, g + 4):
                    sp.dma_start(W2s[:, e], W2[e].rearrange("(c f) d -> f c d", f=P)).then_inc(e_in, 16)

            def save(half, par):
                if live(half, par, 5):
                    b, k, n = turn(half, par, 5)
                    wait(sp, xn2T_ok, b + 1)
                    sp.sem_inc(sp_carry, 1)
                    sp.dma_start(XN2T[:, b, :], xn2T[:, k, :]).then_inc(saved[k], 16)
            pipeline(sp, save, NB + LAGS1, FIRST1, NB)
            for k in range(2):
                sp.wait_ge(saved[k], 16 * NB // 2)
            sp.wait_ge(v2p_ok, NB)

            def move(half, par):
                if live(half, par, 0):
                    b, k, n = turn(half, par, 0)
                    wait(sp, sp_ok, b - 1)
                    sp.sem_inc(sp_carry, 1)
                    sp.dma_start(xs[:, k, :], XN2T[:, b, :]).then_inc(xs_in[k], 16)
                if live(half, par, 4):
                    b, k, n = turn(half, par, 4)
                    wait(sp, ob_ok, b + 1)
                    sp.sem_inc(sp_carry, 1)
                    sp.dma_start(out_rows[:, b, :], ob[:, k, :]).then_inc(stored[k], 16)
            pipeline(sp, move, NB + LAGS2, FIRST2, NB)
            for k in range(2):
                sp.wait_ge(stored[k], 16 * NB // 2)

        @block.gpsimd
        def _(pool):
            made = [0]

            def own(instruction):
                instruction.then_inc(pool_own, 1)
                made[0] += 1
                pool.wait_ge(pool_own, made[0])

            own(pool.memset(ident[:, :], 0.0))
            pool.affine_select(out=ident[:, :], in_=ident[:, :], compare_op=ALU.not_equal, fill=1.0, base=0,
                               pattern=[[-1, P]], channel_multiplier=1).then_inc(ident_ok, 1)
            own(pool.memset(head8[:, :], 1.0))
            for sign in (1, -1):
                own(pool.affine_select(out=head8[:, :], in_=head8[:, :], compare_op=ALU.is_ge, fill=0.0,
                                       base=0 if sign > 0 else DH - 1, pattern=[[-sign * DH, H]],
                                       channel_multiplier=sign))
            own(pool.memset(head16[:, :], 1.0))
            for sign in (1, -1):
                own(pool.affine_select(out=head16[:, :], in_=head16[:, :], compare_op=ALU.is_ge, fill=0.0,
                                       base=0 if sign > 0 else S - 1, pattern=[[-sign * S, P // S]],
                                       channel_multiplier=sign))
            own(pool.memset(sel3[:, :, :], 0.0))
            own(pool.affine_select(out=sel3[:, :, :], in_=sel3[:, :, :], compare_op=ALU.not_equal, fill=1.0,
                                   base=0, pattern=[[-S, P // S], [-1, S]], channel_multiplier=1))
            own(pool.memset(repS[:, :, :], 0.0))
            own(pool.affine_select(out=repS[:, :, :], in_=repS[:, :, :], compare_op=ALU.not_equal, fill=1.0,
                                   base=0, pattern=[[-1, S], [0, NB]], channel_multiplier=1))
            own(pool.memset(epsT[:, :], EPS))
            own(pool.memset(mhalf[:, :], -0.5))
            own(pool.memset(pvm[:, :, :, :], 0.0))
            own(pool.memset(xn[:, :, :, :], 1.0))
            own(pool.memset(xn2[:, :, :, :], 1.0))
            pool.sem_inc(masks_ok, 1)

            def step(half, par):
                if live(half, par, 3):
                    b, k, n = turn(half, par, 3)
                    wait(pool, rz_ok, b + 1)
                    wait(pool, ft_ok, b + 1)
                    wait(pool, tq_ok, b - 1)
                    for j in range(2):
                        last = pool.tensor_tensor(heads(qz[:, k, j, :], DH), heads(ft[:, k, j, 0:P], DH),
                                                  over(rz[:, k, j * H:(j + 1) * H], DH), ALU.mult)
                    last.then_inc(qz_ok, 1)
                if live(half, par, 4):
                    b, k, n = turn(half, par, 4)
                    wait(pool, mv2_ok, b + 1)
                    pool.tensor_tensor(ve2[:, k, :], mv2[:, k, :, 1], epsT[:, :], ALU.add).then_inc(ve2_ok, 1)
                    wait(pool, ve2_ok, b + 1)
                    pool.tensor_tensor(rs2[:, k, :], ve2[:, k, :], mhalf[:, :], ALU.pow).then_inc(rs2_ok, 1)
                if live(half, par, 0):
                    b, k, n = turn(half, par, 0)
                    wait(pool, mv1_ok, b + 1)
                    pool.tensor_tensor(ve1[:, k, :], mv1[:, k, :, 1], epsT[:, :], ALU.add).then_inc(ve1_ok, 1)
                    wait(pool, ve1_ok, b + 1)
                    pool.tensor_tensor(rs1[:, k, :], ve1[:, k, :], mhalf[:, :], ALU.pow).then_inc(rs1_ok, 1)
                    wait(pool, xn_ok, b + 1)
                    pool.tensor_tensor(X[:, b, :].rearrange("p (j d) -> p j d", j=2),
                                       X[:, b, :].rearrange("p (j d) -> p j d", j=2),
                                       under(a_bo_all[:, :], 2), ALU.add).then_inc(xbo_ok, 1)
                if live(half, par, 5):
                    b, k, n = turn(half, par, 5)
                    wait(pool, xn2_ok, b + 1)
                    pool.tensor_tensor(X[:, b, :].rearrange("p (j d) -> p j d", j=2),
                                       X[:, b, :].rearrange("p (j d) -> p j d", j=2),
                                       under(c_bo_all[:, :], 2), ALU.add).then_inc(xcbo_ok, 1)

            for g in range(4):
                pool.wait_ge(x_in[g], 16)
            pool.wait_ge(w_in, 16 * N_SMALL)
            pipeline(pool, step, NB + LAGS1, FIRST1, NB)

            pool.wait_ge(mid_dve, 3)
            pool.tensor_tensor(ve3[:, :], mv3[:, :, 1], epsT[:, :], ALU.add).then_inc(mid_pool, 1)
            pool.wait_ge(mid_pool, 1)
            pool.tensor_tensor(rs3[:, :], ve3[:, :], mhalf[:, :], ALU.pow).then_inc(mid_pool, 1)

            def step2(half, par):
                if live(half, par, 3):
                    b, k, n = turn(half, par, 3)
                    wait(pool, rsm_ok, b + 1)
                    wait(pool, tt_ok, b - 1)
                    for j in range(2):
                        last = pool.tensor_tensor(heads(at[:, k, j * HS:(j + 1) * HS], S),
                                                  heads(ep[:, k, j * HS:(j + 1) * HS], S),
                                                  over(rsm[:, k, j * H:(j + 1) * H], S), ALU.mult)
                    last.then_inc(at_ok, 1)
                if live(half, par, 0):
                    b, k, n = turn(half, par, 0)
                    wait(pool, ap_ok, b - 1)
                    pool.tensor_tensor(heads(BDk[:, k, :], S), under(kT[:, :, b], H), over(head8[:, :], S),
                                       ALU.mult).then_inc(bdk_ok, 1)
                if live(half, par, 2):
                    b, k, n = turn(half, par, 2)
                    wait(pool, vwp_ok, b - 1)
                    pool.tensor_tensor(heads(BDv[:, k, :], S), under(vT[:, :, b], H), over(head8[:, :], S),
                                       ALU.mult).then_inc(bdv_ok, 1)

            pool.wait_ge(kT_ok, 1)
            pool.wait_ge(vT_ok, 1)
            pipeline(pool, step2, NB + LAGS2, FIRST2, NB)

        @block.scalar
        def _(sc):
            for g in range(4):
                sc.dma_start(X[:, 4 * g:4 * g + 4, :], x_rows[:, 4 * g:4 * g + 4, :]).then_inc(x_in[g], 16)
            sc.wait_ge(su_pe, 2)
            sc.activation(fvecT[:, :, :], ps[:, 6, 0:P].rearrange("p (u m) -> p u m", u=2), ACT.Copy)
            sc.wait_ge(su_pe, 3)
            sc.activation(Wt[:, :, :], ps[:, 5, 0:3 * P].rearrange("p (m n) -> p m n", m=3),
                          ACT.Copy).then_inc(su_act, 1)
            sc.wait_ge(su_pe, 4)
            sc.activation(Wproj[:, 0:2 * P], ps[:, 4, 0:2 * P], ACT.Copy, scale=0.25)
            sc.activation(WvP[:, :], ps[:, 4, 2 * P:3 * P], ACT.Copy)
            sc.activation(WoT[:, :], ps[:, 4, 3 * P:4 * P], ACT.Copy)
            sc.wait_ge(su_pe, 5)
            sc.activation(Wproj[:, 2 * P:4 * P], ps[:, 3, 0:2 * P], ACT.Copy, scale=SC)
            sc.wait_ge(su_pe, 7)
            sc.activation(dWvP[:, :], ps[:, 1, 0:P], ACT.Copy)
            sc.wait_ge(su_pe, 8)
            sc.activation(Ad[:, :], ps[:, 0, 0:HS], ACT.Copy).then_inc(su_act, 1)

            def step(half, par):
                if live(half, par, 3):
                    b, k, n = turn(half, par, 3)
                    wait(sc, ex_ok, b + 1)
                    wait(sc, kv_ok, b - 1)
                    wait(sc, qz_ok, b - 1)
                    sc.activation(ft[:, k], ex[:, k], ACT.Exp).then_inc(ft_ok, 1)
                if live(half, par, 2):
                    b, k, n = turn(half, par, 2)
                    wait(sc, proj_ok, b + 1)
                    wait(sc, ss_ok, b - 1)
                    sc.activation(sq[:, k], ps[:, 0:2, 0:2 * P], ACT.Square).then_inc(sq_ok, 1)
                    wait(sc, vp_ok, b + 1)
                    wait(sc, kv_ok, b - 1)
                    sc.activation(Vs[:, k], ps[:, 2, 0:2 * P].rearrange("p (j d) -> p j d", j=2),
                                  ACT.Copy).then_inc(v_ok, 1)
                if live(half, par, 6):
                    b, k, n = turn(half, par, 6)
                    wait(sc, tp_ok, b + 1)
                    wait(sc, pv_ok, b - 1)
                    sc.activation(prT[:, k], ps[:, 5, :].rearrange("p (j m) -> p j m", j=2),
                                  ACT.Copy).then_inc(prT_ok, 1)
                if live(half, par, 3):
                    b, k, n = turn(half, par, 3)
                    wait(sc, mp_ok, b + 1)
                    wait(sc, out_ok, b - 1)
                    sc.activation(Mb[:, k, :], ps[:, 6, P:2 * P], ACT.Copy).then_inc(mb_ok, 1)
                if live(half, par, 5):
                    b, k, n = turn(half, par, 5)
                    wait(sc, v2p_ok, b + 1)
                    wait(sc, pv_ok, b - 1)
                    sc.activation(V2s[:, k], ps[:, 2, 0:2 * P].rearrange("p (j d) -> p j d", j=2),
                                  ACT.Copy).then_inc(v2_ok, 1)
                    wait(sc, nmax_ok, b + 1)
                    wait(sc, tp_ok, b - 1)
                    wait(sc, rps_ok, b - 1)
                    for hf in range(2):
                        last = sc.activation(pr[:, k, hf, :], ps[:, 4, hf * NT:(hf + 1) * NT], ACT.Exp,
                                             bias=nmax[:, k, hf:hf + 1], accum_out=psm[:, k, hf:hf + 1])
                    last.then_inc(pr_ok, 1)
                if live(half, par, 1):
                    b, k, n = turn(half, par, 1)
                    wait(sc, tx_ok, b + 1)
                    wait(sc, vp_ok, b - 1)
                    sc.activation(xnT[:, k, :], ps[:, 3, 0:NT], ACT.Copy).then_inc(xnT_ok, 1)
                if live(half, par, 3):
                    b, k, n = turn(half, par, 3)
                    wait(sc, tq_ok, b + 1)
                    wait(sc, out_ok, b - 1)
                    sc.activation(qzT[:, k, :], ps[:, 7, 0:NT], ACT.Copy).then_inc(qzT_ok, 1)
                if live(half, par, 4):
                    b, k, n = turn(half, par, 4)
                    wait(sc, tx2_ok, b + 1)
                    wait(sc, v2p_ok, b - 1)
                    wait(sc, saved[k], n * 16, NB * 8)
                    sc.activation(xn2T[:, k, :], ps[:, 5, 0:NT], ACT.Copy).then_inc(xn2T_ok, 1)

            pipeline(sc, step, NB + LAGS1, FIRST1, NB)

            sc.wait_ge(mid_pe, 1)
            sc.activation(o1[:, :, :], ps[:, 0, 0:2 * P].rearrange("p (j d) -> p j d", j=2),
                          ACT.Copy).then_inc(mid_act, 1)
            for g in range(S // EG):
                sc.wait_ge(ug_ok, g + 1)
                if g >= 2:
                    sc.wait_ge(sg_ok, g - 1)
                sc.activation(th[:, g % 2], ug[:, g % 2], ACT.Tanh, scale=0.5).then_inc(th_ok, 1)

            def step2(half, par):
                if live(half, par, 4):
                    b, k, n = turn(half, par, 4)
                    wait(sc, tt_ok, b + 1)
                    wait(sc, op_ok, b - 1)
                    sc.activation(atT[:, k], ps[:, 4 + k, :].rearrange("p (h t) -> p h t", h=2),
                                  ACT.Copy).then_inc(atT_ok, 1)
                if live(half, par, 1):
                    b, k, n = turn(half, par, 1)
                    wait(sc, ap_ok, b + 1)
                    wait(sc, sp_ok, b - 1)
                    sc.activation(As[:, k, :], ps[:, k, 0:HS], ACT.Copy).then_inc(a_ok, 1)
                if live(half, par, 3):
                    b, k, n = turn(half, par, 3)
                    wait(sc, vwp_ok, b + 1)
                    wait(sc, op_ok, b - 1)
                    sc.activation(VWs[:, k, :], ps[:, 1 - k, 0:HS], ACT.Copy).then_inc(vw_ok, 1)
                if live(half, par, 2):
                    b, k, n = turn(half, par, 2)
                    wait(sc, sx_ok, b + 1)
                    wait(sc, at_ok, b - 1)
                    wait(sc, sm_ok, b - 1)
                    sc.activation(ep[:, k, :], sx[:, k, :], ACT.Exp).then_inc(ep_ok, 1)

            pipeline(sc, step2, NB + LAGS2, FIRST2, NB)

        @block.vector
        def _(ve):
            ve.wait_ge(masks_ok, 1)
            ve.wait_ge(w_in, 16 * N_SMALL)
            ve.tensor_reduce(selS[:, :], sel3[:, :, :].rearrange("p h s -> p s h"), AX.X, ALU.add)
            ve.tensor_tensor(heads(BDR[:, :], DH), under(Rrep[:, :], H), over(head8[:, :], DH), ALU.mult)
            for m in (AQ, AK, AV):
                ve.tensor_scalar(W[:, m, 0:L], W[:, m, 0:L], W[:, m, L:P], None, ALU.subtract)
            ve.tensor_tensor(slotb[:, :], vec[SLOT:SLOT + S, :], d_bo_all[:, :], ALU.add).then_inc(su_dve, 1)
            ve.wait_ge(su_pe, 1)
            ve.tensor_copy(vecT[:, :], ps[:, 7, 0:NR]).then_inc(su_dve, 1)
            ve.wait_ge(su_dve, 2)
            ve.tensor_copy(W[:, AQ:AV + 1, L], vecT[:, BQ:BV + 1]).then_inc(su_dve, 1)
            ve.wait_ge(su_act, 1)
            for m in range(3):
                last = ve.tensor_scalar(Wt[:, m, 0:L], Wt[:, m, 0:L], Wt[:, m, L:P], None, ALU.subtract)
            last.then_inc(passed, 1)
            ve.wait_ge(passed, 1)
            ve.tensor_copy(Wt[:, :, L], vecT[:, BDK:BCQ + 1])
            ve.wait_ge(su_pe, 6)
            ve.tensor_scalar(qTs[:, :], ps[:, 2, 0:S], vecT[:, BDQ:BDQ + 1], SC, ALU.add,
                             ALU.mult).then_inc(passed, 1)
            ve.wait_ge(passed, 2)
            ve.tensor_tensor(heads(qbd[:, :], S), under(qTs[:, :], H), over(head8[:, :], S),
                             ALU.mult).then_inc(su_dve, 1)
            for g in range(4):
                ve.wait_ge(x_in[g], 16)
            ve.wait_ge(su_act, 2)

            def step(half, par):
                if live(half, par, 0):
                    b, k, n = turn(half, par, 0)
                    for j in range(2):
                        last = ve.bn_stats(st1[:, k, j, :], X[:, b, j * P:(j + 1) * P])
                    last.then_inc(bn1_ok, 1)
                if live(half, par, 4):
                    b, k, n = turn(half, par, 4)
                    wait(ve, out_ok, b + 1)
                    wait(ve, xbo_ok, b + 1)
                    ve.tensor_tensor(X[:, b, :], ps[:, 7, 0:NT], X[:, b, :], ALU.add).then_inc(x2_ok, 1)
                if live(half, par, 0):
                    b, k, n = turn(half, par, 0)
                    wait(ve, bn1_ok, b + 1)
                    wait(ve, rs1_ok, b - 1)
                    ve.sem_inc(dve_carry, 1)
                    for j in range(2):
                        last = ve.bn_aggr(mv1[:, k, j, :], st1[:, k, j, :])
                    last.then_inc(mv1_ok, 1)
                if live(half, par, 4):
                    b, k, n = turn(half, par, 4)
                    wait(ve, x2_ok, b + 1)
                    ve.sem_inc(dve_carry, 1)
                    for j in range(2):
                        last = ve.bn_stats(st2[:, k, j, :], X[:, b, j * P:(j + 1) * P])
                    last.then_inc(bn2_ok, 1)
                if live(half, par, 3):
                    b, k, n = turn(half, par, 3)
                    wait(ve, ft_ok, b + 1)
                    ve.tensor_reduce(den[:, k, :].rearrange("p (j h) -> p j h", j=2),
                                     ft[:, k, :, 0:P].rearrange("p j (h d) -> p j h d", d=DH), AX.X,
                                     ALU.add).then_inc(den_ok, 1)
                if live(half, par, 4):
                    b, k, n = turn(half, par, 4)
                    wait(ve, bn2_ok, b + 1)
                    ve.sem_inc(dve_carry, 1)
                    for j in range(2):
                        last = ve.bn_aggr(mv2[:, k, j, :], st2[:, k, j, :])
                    last.then_inc(mv2_ok, 1)
                if live(half, par, 3):
                    b, k, n = turn(half, par, 3)
                    wait(ve, den_ok, b + 1)
                    ve.tensor_scalar(den2[:, k, :], den[:, k, :], 1e-8, None, ALU.add).then_inc(den2_ok, 1)
                    wait(ve, den2_ok, b + 1)
                    wait(ve, qz_ok, b - 1)
                    ve.reciprocal(rz[:, k, :], den2[:, k, :]).then_inc(rz_ok, 1)
                    wait(ve, kv_ok, b + 1)
                    wait(ve, mp_ok, b - 1)
                    ve.tensor_tensor(heads(kvm[:, k, :], DH), heads(ps[:, 6, 0:P], DH), over(head8[:, :], DH),
                                     ALU.mult).then_inc(kvm_ok, 1)
                if live(half, par, 0):
                    b, k, n = turn(half, par, 0)
                    wait(ve, rs1_ok, b + 1)
                    wait(ve, tx_ok, b - 1)
                    for j in range(2):
                        last = ve.tensor_scalar(xn[:, k, j, 0:L], X[:, b, j * P:j * P + L], mv1[:, k, j, 0:1],
                                                rs1[:, k, j:j + 1], ALU.subtract, ALU.mult)
                    last.then_inc(xn_ok, 1)
                if live(half, par, 4):
                    b, k, n = turn(half, par, 4)
                    wait(ve, rs2_ok, b + 1)
                    wait(ve, tx2_ok, b - 1)
                    for j in range(2):
                        last = ve.tensor_scalar(xn2[:, k, j, 0:L], X[:, b, j * P:j * P + L], mv2[:, k, j, 0:1],
                                                rs2[:, k, j:j + 1], ALU.subtract, ALU.mult)
                    last.then_inc(xn2_ok, 1)
                if live(half, par, 2):
                    b, k, n = turn(half, par, 2)
                    wait(ve, sq_ok, b + 1)
                    ve.tensor_reduce(ss[:, k, :].rearrange("p (j h) -> p j h", j=2),
                                     sq[:, k].rearrange("p j (h d) -> p j h d", d=DH), AX.X,
                                     ALU.add).then_inc(ss_ok, 1)
                    wait(ve, ss_ok, b + 1)
                    wait(ve, ft_ok, b - 1)
                    ve.tensor_tensor(ex[:, k].rearrange("p j (h d) -> p j h d", d=DH),
                                     ps[:, 0:2, 2 * P:4 * P].rearrange("p j (h d) -> p j h d", d=DH),
                                     ss[:, k, :].rearrange("p (j h) -> p j h", j=2).unsqueeze(3)
                                     .broadcast_to([P, 2, 2 * H, DH]), ALU.subtract).then_inc(ex_ok, 1)
                if live(half, par, 5):
                    b, k, n = turn(half, par, 5)
                    wait(ve, s_ok, b + 1)
                    ve.tensor_reduce(nmax[:, k, :], ps[:, 4, :].rearrange("p (h t) -> p h t", h=2), AX.X,
                                     ALU.max, negate=True).then_inc(nmax_ok, 1)
                if live(half, par, 6):
                    b, k, n = turn(half, par, 6)
                    wait(ve, pr_ok, b + 1)
                    ve.reciprocal(rps[:, k, :], psm[:, k, :]).then_inc(rps_ok, 1)
                    wait(ve, rps_ok, b + 1)
                    wait(ve, pv_ok, b + 1)
                    wait(ve, sel_ok, b - 1)
                    for hf in range(2):
                        last = ve.scalar_tensor_tensor(
                            out=heads(pvm[:, k, hf, hf * 64:hf * 64 + 64], DH),
                            in0=heads(ps[:, 6, 2 * P + hf * 64:2 * P + hf * 64 + 64], DH),
                            scalar=rps[:, k, hf:hf + 1], in1=over(head16[:, :], DH), op0=ALU.mult, op1=ALU.mult)
                    last.then_inc(pvm_ok, 1)
                    wait(ve, sel_ok, b + 1)
                    ve.tensor_scalar(aoT[:, :, b], ps[:, 6, 3 * P:3 * P + S], 1.0, None,
                                     ALU.mult).then_inc(ao_ok, 1)

            pipeline(ve, step, NB + LAGS1, FIRST1, NB)

            ve.wait_ge(mid_act, 1)
            for j in range(2):
                last = ve.bn_stats(st3[:, j, :], o1[:, j, :])
            last.then_inc(mid_dve, 1)
            ve.wait_ge(mid_dve, 1)
            ve.bn_aggr(mv3[:, 0, :], st3[:, 0, :]).then_inc(mid_dve, 1)
            ve.bn_aggr(mv3[:, 1, :], st3[:, 1, :]).then_inc(mid_dve, 1)
            ve.wait_ge(mid_pe, 2)
            ve.tensor_tensor(o1b[:, :, :], ps[:, 1, 0:2 * P].rearrange("p (s b) -> p s b", b=NB),
                             over(vecT[:, B2:B2 + S], NB), ALU.add)
            ve.wait_ge(mid_pool, 2)
            for j in range(2):
                last = ve.tensor_scalar(xh[:, j, :], o1[:, j, :], mv3[:, j, 0:1], rs3[:, j:j + 1], ALU.subtract,
                                        ALU.mult)
            last.then_inc(mid_dve, 1)
            ve.wait_ge(mid_pe, 3)
            ve.tensor_tensor(hg[:, :, :], ps[:, 2, 0:2 * P].rearrange("p (s b) -> p s b", b=NB),
                             over(vecT[:, GAIN:GAIN + S], NB), ALU.mult).then_inc(mid_dve, 1)
            ve.wait_ge(mid_dve, 5)
            ve.tensor_tensor(hT[:, :, :], hg[:, :, :], over(vecT[:, SHIFT:SHIFT + S], NB),
                             ALU.add).then_inc(mid_dve, 1)
            n = EG * FC

            def gate(g):
                k = g % 2
                ve.wait_ge(th_ok, g + 1)
                if g >= 2:
                    ve.wait_ge(act_ok, g - 1)
                ve.scalar_tensor_tensor(out=sg[:, k], in0=th[:, k], scalar=1.0, in1=ug[:, k], op0=ALU.add,
                                        op1=ALU.mult).then_inc(sg_ok, 1)
                ve.wait_ge(sg_ok, g + 1)
                if g >= 2:
                    ve.wait_ge(y_ok, g - 1)
                ve.tensor_tensor(act[:, k].rearrange("p e c b -> p (e c b)"), sg[:, k, 0, :], sg[:, k, 1, :],
                                 ALU.mult).then_inc(act_ok, 1)

            for g in range(S // EG):
                k = g % 2
                ve.wait_ge(up_ok, g + 1)
                if g >= 2:
                    ve.wait_ge(sg_ok, g - 1)
                ve.tensor_tensor(ug[:, k].rearrange("p u (n b) -> p u n b", b=NB),
                                 ps[:, 3 + k, :].rearrange("p (u n b) -> p u n b", u=2, b=NB),
                                 fvecT[:, :, g * n:(g + 1) * n].unsqueeze(3).broadcast_to([P, 2, n, NB]),
                                 ALU.add).then_inc(ug_ok, 1)
                if g >= 1:
                    gate(g - 1)
            gate(S // EG - 1)
            ve.wait_ge(y_ok, S // EG)
            ve.scalar_tensor_tensor(out=o2T[:, :], in0=ps[:, 5, 0:2 * P], scalar=0.25,
                                    in1=o1b[:, :, :].rearrange("p s b -> p (s b)"), op0=ALU.mult,
                                    op1=ALU.add).then_inc(o2_ok, 1)
            ve.wait_ge(kvp_ok, 1)
            ve.tensor_scalar(kT[:, :, :].rearrange("p s b -> p (s b)"), ps[:, 6, 0:2 * P],
                             vecT[:, BCK:BCK + 1], SC, ALU.add, ALU.mult).then_inc(kT_ok, 1)
            ve.wait_ge(kvp_ok, 2)
            ve.tensor_scalar(vT[:, :, :].rearrange("p s b -> p (s b)"), ps[:, 7, 0:2 * P],
                             vecT[:, BCV:BCV + 1], None, ALU.add).then_inc(vT_ok, 1)

            def step2(half, par):
                if live(half, par, 3):
                    b, k, n = turn(half, par, 3)
                    wait(ve, ep_ok, b + 1)
                    ve.tensor_reduce(sm[:, k, :], heads(ep[:, k, :], S), AX.X, ALU.add).then_inc(sm_ok, 1)
                    wait(ve, sm_ok, b + 1)
                    wait(ve, at_ok, b - 1)
                    ve.reciprocal(rsm[:, k, :], sm[:, k, :]).then_inc(rsm_ok, 1)
                if live(half, par, 2):
                    b, k, n = turn(half, par, 2)
                    wait(ve, sp_ok, b + 1)
                    ve.tensor_reduce(mx[:, k, :], heads(ps[:, 2 + k, :], S), AX.X, ALU.max).then_inc(mx_ok, 1)
                    wait(ve, mx_ok, b + 1)
                    wait(ve, ep_ok, b - 1)
                    ve.tensor_tensor(heads(sx[:, k, :], S), heads(ps[:, 2 + k, :], S), over(mx[:, k, :], S),
                                     ALU.subtract).then_inc(sx_ok, 1)
                if live(half, par, 4):
                    b, k, n = turn(half, par, 4)
                    wait(ve, op_ok, b + 1)
                    wait(ve, stored[k], n * 16, NB * 8)
                    ve.tensor_tensor(ob[:, k, :], ps[:, 6 + k, 0:NT], X[:, b, :], ALU.add).then_inc(ob_ok, 1)

            ve.wait_ge(xcbo_ok, NB)
            pipeline(ve, step2, NB + LAGS2, FIRST2, NB)

        @block.tensor
        def _(pe):
            pe.wait_ge(ident_ok, 1)
            pe.wait_ge(w_in, 16 * N_SMALL)
            pe.transpose(ps[:, 7, 0:NR], vec[:, :], ident[0:NR, 0:NR]).then_inc(su_pe, 1)
            pe.transpose(ps[:, 6, 0:P], fvec[:, :], ident[:, :]).then_inc(su_pe, 1)
            for n, m in enumerate((DK, DV, CQ)):
                last = pe.transpose(ps[:, 5, n * P:(n + 1) * P], W[:, m, :], ident[:, :])
            last.then_inc(su_pe, 1)
            pe.wait_ge(su_dve, 3)
            for n, m in enumerate((AQ, AK, AV, AO)):
                last = pe.transpose(ps[:, 4, n * P:(n + 1) * P], W[:, m, :], ident[:, :])
            last.then_inc(su_pe, 1)
            for n, m in enumerate((AQ, AK)):
                last = pe.matmul(ps[:, 3, n * P:(n + 1) * P], W[:, m, :], BDR[:, :], start=True, stop=True)
            last.then_inc(su_pe, 1)
            pe.matmul(ps[:, 2, 0:S], W[:, DQ, :], vecT[:, SLOT:SLOT + S], start=True,
                      stop=True).then_inc(su_pe, 1)
            pe.wait_ge(su_dve, 4)
            pe.transpose(ps[:, 1, 0:P], Wt[:, 1, :], ident[:, :]).then_inc(su_pe, 1)
            pe.matmul(ps[:, 0, 0:HS], Wt[:, 0, :], qbd[:, :], start=True, stop=True).then_inc(su_pe, 1)
            pe.wait_ge(su_act, 2)

            def step(half, par):
                if live(half, par, 4):
                    b, k, n = turn(half, par, 4)
                    wait(pe, mb_ok, b + 1)
                    wait(pe, qzT_ok, b + 1)
                    for j in range(2):
                        last = pe.matmul(ps[:, 7, j * P:(j + 1) * P], qzT[:, k, j * P:(j + 1) * P], Mb[:, k, :],
                                         start=True, stop=True)
                    last.then_inc(out_ok, 1)
                if live(half, par, 2):
                    b, k, n = turn(half, par, 2)
                    wait(pe, xnT_ok, b + 1)
                    wait(pe, ex_ok, b)
                    for j in range(2):
                        last = pe.matmul(ps[:, j, :], xnT[:, k, j * P:(j + 1) * P], Wproj[:, :], start=True,
                                         stop=True)
                    last.then_inc(proj_ok, 1)
                    wait(pe, v2_ok, b - 3)
                    for j in range(2):
                        last = pe.matmul(ps[:, 2, j * P:(j + 1) * P], xnT[:, k, j * P:(j + 1) * P], WvP[:, :],
                                         start=True, stop=True)
                    last.then_inc(vp_ok, 1)
                if live(half, par, 3):
                    b, k, n = turn(half, par, 3)
                    wait(pe, ft_ok, b + 1)
                    wait(pe, v_ok, b + 1)
                    wait(pe, ao_ok, b - 3)
                    for j in range(2):
                        last = pe.matmul(ps[:, 6, 0:P], Vs[:, k, j, :], ft[:, k, j, P:2 * P], start=(j == 0),
                                         stop=(j == 1))
                    last.then_inc(kv_ok, 1)
                if live(half, par, 6):
                    b, k, n = turn(half, par, 6)
                    wait(pe, pr_ok, b + 1)
                    wait(pe, xn2T_ok, b + 2)
                    for j in range(2):
                        for hf in range(2):
                            last = pe.transpose(ps[:, 5, j * HS + hf * P:j * HS + (hf + 1) * P],
                                                pr[:, k, hf, j * P:(j + 1) * P], ident[:, :])
                    last.then_inc(tp_ok, 1)
                if live(half, par, 5):
                    b, k, n = turn(half, par, 5)
                    wait(pe, xn2T_ok, b + 1)
                    wait(pe, pr_ok, b)
                    for hf in range(2):
                        last = pe.matmul(ps[:, 4, hf * NT:(hf + 1) * NT], Ad[:, hf * P:(hf + 1) * P],
                                         xn2T[:, k, :], start=True, stop=True)
                    last.then_inc(s_ok, 1)
                    wait(pe, v_ok, b + 4)
                    wait(pe, v2_ok, b)
                    for j in range(2):
                        last = pe.matmul(ps[:, 2, j * P:(j + 1) * P], xn2T[:, k, j * P:(j + 1) * P], dWvP[:, :],
                                         start=True, stop=True)
                    last.then_inc(v2p_ok, 1)
                if live(half, par, 3):
                    b, k, n = turn(half, par, 3)
                    wait(pe, kvm_ok, b + 1)
                    pe.matmul(ps[:, 6, P:2 * P], kvm[:, k, :], WoT[:, :], start=True, stop=True).then_inc(mp_ok, 1)
                if live(half, par, 6):
                    b, k, n = turn(half, par, 6)
                    wait(pe, prT_ok, b + 1)
                    wait(pe, v2_ok, b + 1)
                    wait(pe, mb_ok, b + 4)
                    wait(pe, ao_ok, b)
                    for hf in range(2):
                        for j in range(2):
                            last = pe.matmul(ps[:, 6, 2 * P + hf * 64:2 * P + hf * 64 + 64],
                                             prT[:, k, j, hf * P:(hf + 1) * P],
                                             V2s[:, k, j, hf * 64:hf * 64 + 64], start=(j == 0), stop=(j == 1))
                    last.then_inc(pv_ok, 1)
                if live(half, par, 1):
                    b, k, n = turn(half, par, 1)
                    wait(pe, xn_ok, b + 1)
                    wait(pe, xnT_ok, b)
                    for j in range(2):
                        last = pe.transpose(ps[:, 3, j * P:(j + 1) * P], xn[:, k, j, :], ident[:, :])
                    last.then_inc(tx_ok, 1)
                if live(half, par, 3):
                    b, k, n = turn(half, par, 3)
                    wait(pe, qz_ok, b + 1)
                    wait(pe, x2_ok, b)
                    for j in range(2):
                        last = pe.transpose(ps[:, 7, j * P:(j + 1) * P], qz[:, k, j, :], ident[:, :])
                    last.then_inc(tq_ok, 1)
                if live(half, par, 4):
                    b, k, n = turn(half, par, 4)
                    wait(pe, xn2_ok, b + 1)
                    wait(pe, prT_ok, b - 1)
                    for j in range(2):
                        last = pe.transpose(ps[:, 5, j * P:(j + 1) * P], xn2[:, k, j, :], ident[:, :])
                    last.then_inc(tx2_ok, 1)
                if live(half, par, 6):
                    b, k, n = turn(half, par, 6)
                    wait(pe, pvm_ok, b + 1)
                    for hf in range(2):
                        last = pe.matmul(ps[:, 6, 3 * P:3 * P + S], pvm[:, k, hf, :], selS[:, :],
                                         start=(hf == 0), stop=(hf == 1))
                    last.then_inc(sel_ok, 1)

            pipeline(pe, step, NB + LAGS1, FIRST1, NB)

            pe.wait_ge(ao_ok, NB)
            ao = aoT[:, :, :].rearrange("p s b -> p (s b)")
            rep = repS[:, :, :].rearrange("p s b -> p (s b)")
            for j in range(2):
                pe.matmul(ps[:, 0, j * P:(j + 1) * P], ao[:, j * P:(j + 1) * P], W[:, DO, :], start=True, stop=False)
                last = pe.matmul(ps[:, 0, j * P:(j + 1) * P], rep[:, j * P:(j + 1) * P], slotb[:, :], start=False,
                                 stop=True)
            last.then_inc(mid_pe, 1)
            pe.wait_ge(mid_act, 1)
            for j in range(2):
                last = pe.transpose(ps[:, 1, j * P:(j + 1) * P], o1[:, j, :], ident[:, :])
            last.then_inc(mid_pe, 1)
            pe.wait_ge(mid_dve, 4)
            for j in range(2):
                last = pe.transpose(ps[:, 2, j * P:(j + 1) * P], xh[:, j, :], ident[:, :])
            last.then_inc(mid_pe, 1)
            pe.wait_ge(mid_dve, 6)
            pe.wait_ge(e_in, 16 * (8 + S))

            def experts_in(g):
                if g >= 2:
                    pe.wait_ge(ug_ok, g - 1)
                for e in range(g * EG, (g + 1) * EG):
                    for u, w in enumerate((W1s, Wgs)):
                        for c in range(FC):
                            at0 = ((u * EG + e % EG) * FC + c) * NB
                            last = pe.matmul(ps[:, 3 + g % 2, at0:at0 + NB], w[:, e, c * P:(c + 1) * P],
                                             hT[:, e, :], start=True, stop=True)
                last.then_inc(up_ok, 1)

            def experts_out(g):
                pe.wait_ge(act_ok, g + 1)
                for e in range(g * EG, (g + 1) * EG):
                    for c in range(FC):
                        last = pe.matmul(ps[:, 5, e * NB:(e + 1) * NB], W2s[:, e, c, :], act[:, g % 2, e % EG, c, :],
                                         start=(c == 0), stop=(c == FC - 1))
                last.then_inc(y_ok, 1)

            for g in range(S // EG):
                experts_in(g)
                if g >= 1:
                    experts_out(g - 1)
            experts_out(S // EG - 1)
            pe.wait_ge(o2_ok, 1)
            pe.matmul(ps[:, 6, 0:2 * P], W[:, CK, :], o2T[:, :], start=True, stop=True).then_inc(kvp_ok, 1)
            pe.matmul(ps[:, 7, 0:2 * P], W[:, CV, :], o2T[:, :], start=True, stop=True).then_inc(kvp_ok, 1)

            def step2(half, par):
                if live(half, par, 2):
                    b, k, n = turn(half, par, 2)
                    wait(pe, a_ok, b + 1)
                    wait(pe, xs_in[k], (n + 1) * 16, NB * 8)
                    wait(pe, sx_ok, b - 1)
                    for j in range(2):
                        last = pe.matmul(ps[:, 2 + k, j * HS:(j + 1) * HS], xs[:, k, j * P:(j + 1) * P],
                                         As[:, k, :], start=True, stop=True)
                    last.then_inc(sp_ok, 1)
                if live(half, par, 1):
                    b, k, n = turn(half, par, 1)
                    wait(pe, bdk_ok, b + 1)
                    wait(pe, a_ok, b - 1)
                    wait(pe, vw_ok, b - 2)
                    pe.matmul(ps[:, k, 0:HS], Wt[:, 2, :], BDk[:, k, :], start=True, stop=True).then_inc(ap_ok, 1)
                if live(half, par, 3):
                    b, k, n = turn(half, par, 3)
                    wait(pe, bdv_ok, b + 1)
                    wait(pe, a_ok, b + 2)
                    wait(pe, vw_ok, b - 1)
                    for hf in range(2):
                        last = pe.matmul(ps[:, 1 - k, hf * P:(hf + 1) * P], BDv[:, k, hf * P:(hf + 1) * P],
                                         W[:, CO, :], start=True, stop=True)
                    last.then_inc(vwp_ok, 1)
                if live(half, par, 4):
                    b, k, n = turn(half, par, 4)
                    wait(pe, atT_ok, b + 1)
                    wait(pe, ob_ok, b - 1)
                    for j in range(2):
                        for hf in range(2):
                            last = pe.matmul(ps[:, 6 + k, j * P:(j + 1) * P], atT[:, k, hf, j * P:(j + 1) * P],
                                             VWs[:, k, hf * P:(hf + 1) * P], start=(hf == 0),
                                             stop=(hf == 1))
                    last.then_inc(op_ok, 1)
                if live(half, par, 3):
                    b, k, n = turn(half, par, 3)
                    wait(pe, at_ok, b + 1)
                    wait(pe, atT_ok, b - 1)
                    for j in range(2):
                        for hf in range(2):
                            last = pe.transpose(ps[:, 4 + k, hf * NT + j * P:hf * NT + (j + 1) * P],
                                                at[:, k, j * HS + hf * P:j * HS + (hf + 1) * P], ident[:, :])
                    last.then_inc(tt_ok, 1)

            pipeline(pe, step2, NB + LAGS2, FIRST2, NB)


_INS = ['L0_attn_x', 'L0_attn_Wq', 'L0_attn_bq', 'L0_attn_Wk', 'L0_attn_bk', 'L0_attn_Wv', 'L0_attn_bv',
        'L0_attn_Wo', 'L0_attn_bo', 'L0_attn_R', 'L0_ffn_slot_query', 'L0_ffn_d_Wq', 'L0_ffn_d_Wk', 'L0_ffn_d_Wv',
        'L0_ffn_d_Wo', 'L0_ffn_d_bq', 'L0_ffn_d_bk', 'L0_ffn_d_bv', 'L0_ffn_d_bo', 'L0_ffn_c_Wq', 'L0_ffn_c_Wk',
        'L0_ffn_c_Wv', 'L0_ffn_c_Wo', 'L0_ffn_c_bq', 'L0_ffn_c_bk', 'L0_ffn_c_bv', 'L0_ffn_c_bo', 'L0_ffn_e_ln_g',
        'L0_ffn_e_ln_b', 'L0_ffn_e_W1', 'L0_ffn_e_b1', 'L0_ffn_e_Wg', 'L0_ffn_e_bg', 'L0_ffn_e_W2', 'L0_ffn_e_b2']
_OUTS = [((16, 256, 128), 'float32')]


def kernel(**inputs):
    import numpy as _np
    import concourse.bacc as _bacc
    from concourse import mybir as _mybir
    from concourse.bass_utils import run_bass_kernel_spmd as _run

    nc = _bacc.Bacc("TRN2", target_bir_lowering=False, num_devices=1)
    arrays, args = {}, []
    for name in _INS:
        a = _np.ascontiguousarray(inputs[name])
        arrays[f"in_{name}_dram"] = a
        args.append(nc.dram_tensor(f"in_{name}_dram", a.shape, _mybir.dt.from_np(a.dtype), kind="ExternalInput").ap())
    for i, (shape, dtype) in enumerate(_OUTS):
        dt = _mybir.dt.from_np(_np.dtype(dtype))
        args.append(nc.dram_tensor(f"out_{i}_dram", shape, dt, kind="ExternalOutput").ap())
    build(nc, *args)
    r = _run(nc, [arrays], core_ids=[0])
    got = tuple(r.results[0][f"out_{i}_dram"] for i in range(len(_OUTS)))
    return got[0]
```

```python
from contextlib import ExitStack

import numpy as np
import concourse.bass as bass
from concourse import mybir

F32 = mybir.dt.float32
ACT = mybir.ActivationFunctionType
ALU = mybir.AluOpType
AX = mybir.AxisListType

P = 128
NB = 16
NT = 256
H = 16
DH = P // H
S = 16
HS = H * S
FC = 4
F = FC * P
EG = 4
G = S // EG
Q = P // EG
L = P - 1
EPS = 1e-5
SC = float(1.0 / np.sqrt(DH))

AQ, AK, AV, AO, DK, DV, CQ, DQ, DO, CK, CV, CO = range(12)
SLOT, GAIN, SHIFT, B2, BIAS = 0, 16, 32, 48, 64
BQ, BK, BV, BDK, BDV, BCQ, BDQ, BCK, BCV = range(BIAS, BIAS + 9)
NR = BIAS + 9


def turn(half, par, lag):
    return half * 2 + (par - lag), (par - lag) % 2, half + (par - lag) // 2


def live(half, par, lag):
    return not isinstance(half, int) or 0 <= 2 * half + par - lag < NB


def wait(eng, sem, n, most=NB):
    if isinstance(n, int):
        n = min(n, most)
        if n <= 0:
            return
    eng.wait_ge(sem, n)


def pipeline(eng, step, steps, first, last):
    for t in range(first):
        step(t // 2, t % 2)
    with eng.Fori(0, (last - first) // 2) as i:
        step(i + first // 2, 0)
        step(i + first // 2, 1)
    for t in range(last, steps):
        step(t // 2, t % 2)


LAGS1, FIRST1 = 6, 8
LAGS2, FIRST2 = 5, 6


def build(nc, x, a_Wq, a_bq, a_Wk, a_bk, a_Wv, a_bv, a_Wo, a_bo, R, slot, d_Wq, d_Wk, d_Wv, d_Wo,
          d_bq, d_bk, d_bv, d_bo, c_Wq, c_Wk, c_Wv, c_Wo, c_bq, c_bk, c_bv, c_bo, ln_g, ln_b,
          W1, b1, Wg, bg, W2, b2, out):
    ctx = ExitStack()
    with ctx:
        def sb(name, *shape):
            return ctx.enter_context(nc.sbuf_tensor(name, list(shape), F32))

        def sem(name):
            return ctx.enter_context(nc.semaphore(name))

        X = sb("X", P, NB, NT)
        XN2T = sb("XN2T", P, NB, NT)
        W = sb("W", P, 12, P)
        W1s = sb("W1s", P, S, FC * P)
        Wgs = sb("Wgs", P, S, FC * P)
        W2s = sb("W2s", P, S, FC, P)
        vec = sb("vec", NR, P)
        vecT = sb("vecT", P, NR)
        fvec = sb("fvec", S, 2, F)
        a_bo_all = sb("a_bo_all", P, P)
        c_bo_all = sb("c_bo_all", P, P)
        d_bo_all = sb("d_bo_all", S, P)
        Rrep = sb("Rrep", P, DH)
        ident = sb("ident", P, P)
        head8 = sb("head8", P, H)
        head16 = sb("head16", P, P // S)
        sel3 = sb("sel3", P, P // S, S)
        selS = sb("selS", P, S)
        repS = sb("repS", S, G, P)
        epsT = sb("epsT", P, G)
        mhalf = sb("mhalf", P, G)
        Wt = sb("Wt", P, 3, P)
        Wproj = sb("Wproj", P, 4 * P)
        WvP = sb("WvP", P, P)
        WoT = sb("WoT", P, P)
        BDR = sb("BDR", P, P)
        dWvP = sb("dWvP", P, P)
        qTs = sb("qTs", P, S)
        qbd = sb("qbd", P, HS)
        Ad = sb("Ad", P, HS)
        slotb = sb("slotb", S, P)
        st1 = sb("st1", P, 2, 2, 6)
        mv1 = sb("mv1", P, 2, 2, 2)
        ve1 = sb("ve1", P, 2, 2)
        rs1 = sb("rs1", P, 2, 2)
        xn = sb("xn", P, 2, 2, P)
        xnT = sb("xnT", P, 2, NT)
        sq = sb("sq", P, 2, 2, 2 * P)
        ss = sb("ss", P, 2, 4 * H)
        ex = sb("ex", P, 2, 2, 2 * P)
        ft = sb("ft", P, 2, 2, 2 * P)
        Vs = sb("Vs", P, 2, 2, P)
        den = sb("den", P, 2, 2 * H)
        den2 = sb("den2", P, 2, 2 * H)
        rz = sb("rz", P, 2, 2 * H)
        qz = sb("qz", P, 2, 2, P)
        qzT = sb("qzT", P, 2, NT)
        kvm = sb("kvm", P, 2, P)
        Mb = sb("Mb", P, 2, P)
        st2 = sb("st2", P, 2, 2, 6)
        mv2 = sb("mv2", P, 2, 2, 2)
        ve2 = sb("ve2", P, 2, 2)
        rs2 = sb("rs2", P, 2, 2)
        xn2 = sb("xn2", P, 2, 2, P)
        xn2T = sb("xn2T", P, 2, NT)
        nmax = sb("nmax", P, 2, 2)
        pr = sb("pr", P, 2, 2, NT)
        psm = sb("psm", P, 2, 2)
        rps = sb("rps", P, 2, 2)
        prT = sb("prT", P, 2, 2, HS)
        V2s = sb("V2s", P, 2, 2, P)
        pvm = sb("pvm", P, 2, 2, P)
        aoT = sb("aoT", P, S, Q)
        st3 = sb("st3", P, G, 6)
        mv3 = sb("mv3", P, G, 2)
        ve3 = sb("ve3", P, G)
        rs3 = sb("rs3", P, G)
        xh = xn[:, :, :, :].rearrange("p k j d -> p (k j) d")
        hg = sb("hg", P, S, NB)
        hT = sb("hT", P, S, Q)
        flat3 = "p k j m -> p (k j m)"
        th = [t[:, :, :, :].rearrange(flat3).rearrange("p (u f) -> p u f", u=2) for t in (ft, ex)]
        sg = [t[:, :, :, :].rearrange(flat3).rearrange("p (u f) -> p u f", u=2) for t in (pr, sq)]
        act = sb("act", P, 2, F)
        actT = prT[:, :, :, :].rearrange("p k j m -> p k (j m)").rearrange("p k (c m) -> p k c m", c=FC)
        o2 = xn2[:, :, :, :].rearrange("p k j d -> p (k j) d")
        o2T = sb("o2T", P, S * NB)
        kT = sb("kT", P, S, NB)
        vT = sb("vT", P, S, NB)
        xs = xn2T
        BDk = xnT
        BDv = qzT
        flat = "p k j m -> p k (j m)"
        As = sq[:, :, 0, :]
        VWs = sq[:, :, 1, :]
        sx = ex[:, :, :, :].rearrange(flat)
        ep = ft[:, :, :, :].rearrange(flat)
        at = pr[:, :, :, :].rearrange(flat)
        atT = prT
        mx = sb("mx", P, 2, 2 * H)
        sm = sb("sm", P, 2, 2 * H)
        rsm = sb("rsm", P, 2, 2 * H)
        ob = V2s[:, :, :, :].rearrange(flat)

        ps = ctx.enter_context(nc.psum_tensor("ps", [P, 8, 512], F32))

        x_in = [sem(f"x_in{g}") for g in range(4)]
        w_in, e_in = sem("w_in"), sem("e_in")
        pool_own, ident_ok, masks_ok = sem("pool_own"), sem("ident_ok"), sem("masks_ok")
        su_pe, su_act, su_dve = sem("su_pe"), sem("su_act"), sem("su_dve")
        bn1_ok, mv1_ok, ve1_ok, rs1_ok, xn_ok = (sem(n) for n in ("bn1_ok", "mv1_ok", "ve1_ok", "rs1_ok", "xn_ok"))
        xbo_ok = sem("xbo_ok")
        tx_ok, xnT_ok, proj_ok, vp_ok, v_ok = (sem(n) for n in ("tx_ok", "xnT_ok", "proj_ok", "vp_ok", "v_ok"))
        sq_ok, ss_ok, ex_ok, ft_ok = (sem(n) for n in ("sq_ok", "ss_ok", "ex_ok", "ft_ok"))
        den_ok, den2_ok, rz_ok, qz_ok = (sem(n) for n in ("den_ok", "den2_ok", "rz_ok", "qz_ok"))
        kv_ok, kvm_ok, mb_ok = (sem(n) for n in ("kv_ok", "kvm_ok", "mb_ok"))
        tq_ok, qzT_ok, out_ok, x2_ok = (sem(n) for n in ("tq_ok", "qzT_ok", "out_ok", "x2_ok"))
        bn2_ok, mv2_ok, ve2_ok, rs2_ok, xn2_ok = (sem(n) for n in ("bn2_ok", "mv2_ok", "ve2_ok", "rs2_ok", "xn2_ok"))
        tx2_ok, xn2T_ok, s_ok, nmax_ok = (sem(n) for n in ("tx2_ok", "xn2T_ok", "s_ok", "nmax_ok"))
        v2p_ok, v2_ok, pr_ok, tp_ok, prT_ok = (sem(n) for n in ("v2p_ok", "v2_ok", "pr_ok", "tp_ok", "prT_ok"))
        pv_ok, rps_ok, pvm_ok, sel_ok, ao_ok = (sem(n) for n in ("pv_ok", "rps_ok", "pvm_ok", "sel_ok", "ao_ok"))
        xcbo_ok = sem("xcbo_ok")
        passed, dve_carry, sp_carry = sem("passed"), sem("dve_carry"), sem("sp_carry")
        mid_pe, mid_dve, mid_pool = sem("mid_pe"), sem("mid_dve"), sem("mid_pool")
        up_ok, th_ok, sg_ok, act_ok = (sem(n) for n in ("up_ok", "th_ok", "sg_ok", "act_ok"))
        ta_ok, actT_ok, y_ok, o2s_ok, to_ok = (sem(n) for n in ("ta_ok", "actT_ok", "y_ok", "o2s_ok", "to_ok"))
        o2_ok, kvp_ok, kT_ok, vT_ok = (sem(n) for n in ("o2_ok", "kvp_ok", "kT_ok", "vT_ok"))
        saved = [sem("saved0"), sem("saved1")]
        xs_in = [sem("xs_in0"), sem("xs_in1")]
        stored = [sem("stored0"), sem("stored1")]
        bdk_ok, bdv_ok, ap_ok, a_ok = (sem(n) for n in ("bdk_ok", "bdv_ok", "ap_ok", "a_ok"))
        vwp_ok, vw_ok = sem("vwp_ok"), sem("vw_ok")
        sp_ok, mx_ok, sx_ok, ep_ok = (sem(n) for n in ("sp_ok", "mx_ok", "sx_ok", "ep_ok"))
        sm_ok, rsm_ok, at_ok, tt_ok, atT_ok = (sem(n) for n in ("sm_ok", "rsm_ok", "at_ok", "tt_ok", "atT_ok"))
        op_ok, ob_ok = sem("op_ok"), sem("ob_ok")

        x_rows = x.rearrange("b (p j) d -> p b (j d)", j=2)
        out_rows = out.rearrange("b (p j) d -> p b (j d)", j=2)

        def over(ap, n):
            return ap.unsqueeze(2).broadcast_to([ap.shape[0], ap.shape[1], n])

        def under(ap, n):
            return ap.unsqueeze(1).broadcast_to([ap.shape[0], n, ap.shape[1]])

        def heads(ap, n):
            return ap.rearrange("p (m n) -> p m n", n=n)

        block = ctx.enter_context(nc.Block())

        N_SMALL = 12 + 4 + 9 + 2 + 4

        @block.sync
        def _(sp):
            for m, w in enumerate((a_Wq, a_Wk, a_Wv, a_Wo, d_Wk, d_Wv, c_Wq, d_Wq, d_Wo, c_Wk, c_Wv, c_Wo)):
                sp.dma_start(W[:, m, :], w).then_inc(w_in, 16)
            for r, t in ((SLOT, slot.rearrange("o s d -> (o s) d")), (GAIN, ln_g), (SHIFT, ln_b), (B2, b2)):
                sp.dma_start(vec[r:r + S, :], t).then_inc(w_in, 16)
            for r, t in ((BQ, a_bq), (BK, a_bk), (BV, a_bv), (BDK, d_bk), (BDV, d_bv), (BCQ, c_bq),
                         (BDQ, d_bq), (BCK, c_bk), (BCV, c_bv)):
                sp.dma_start(vec[r:r + 1, :], t.rearrange("(o d) -> o d", o=1)).then_inc(w_in, 16)
            for u, t in enumerate((b1, bg)):
                sp.dma_start(fvec[:, u, :], t).then_inc(w_in, 16)
            sp.dma_start(a_bo_all[:, :], a_bo.partition_broadcast(P)).then_inc(w_in, 16)
            sp.dma_start(c_bo_all[:, :], c_bo.partition_broadcast(P)).then_inc(w_in, 16)
            sp.dma_start(d_bo_all[:, :], d_bo.partition_broadcast(S)).then_inc(w_in, 16)
            sp.dma_start(Rrep[:, :], R.unsqueeze(0).broadcast_to([H, DH, DH])).then_inc(w_in, 16)
            for g in range(0, S, 4):
                sp.dma_start(W1s[:, g:g + 4, :], W1[g:g + 4].rearrange("e d f -> d e f")).then_inc(e_in, 16)
                sp.dma_start(Wgs[:, g:g + 4, :], Wg[g:g + 4].rearrange("e d f -> d e f")).then_inc(e_in, 16)
                for e in range(g, g + 4):
                    sp.dma_start(W2s[:, e], W2[e].rearrange("(c f) d -> f c d", f=P)).then_inc(e_in, 16)

            def save(half, par):
                if live(half, par, 4):
                    b, k, n = turn(half, par, 4)
                    wait(sp, xn2T_ok, b + 1)
                    sp.sem_inc(sp_carry, 1)
                    sp.dma_start(XN2T[:, b, :], xn2T[:, k, :]).then_inc(saved[k], 16)
            pipeline(sp, save, NB + LAGS1, FIRST1, NB)
            for k in range(2):
                sp.wait_ge(saved[k], 16 * NB // 2)
            sp.wait_ge(v2p_ok, NB)

            def move(half, par):
                if live(half, par, 0):
                    b, k, n = turn(half, par, 0)
                    wait(sp, sp_ok, b - 1)
                    sp.sem_inc(sp_carry, 1)
                    sp.dma_start(xs[:, k, :], XN2T[:, b, :]).then_inc(xs_in[k], 16)
                if live(half, par, 4):
                    b, k, n = turn(half, par, 4)
                    wait(sp, ob_ok, b + 1)
                    sp.sem_inc(sp_carry, 1)
                    sp.dma_start(out_rows[:, b, :], ob[:, k, :]).then_inc(stored[k], 16)
            pipeline(sp, move, NB + LAGS2, FIRST2, NB)
            for k in range(2):
                sp.wait_ge(stored[k], 16 * NB // 2)

        @block.gpsimd
        def _(pool):
            made = [0]

            def own(instruction):
                instruction.then_inc(pool_own, 1)
                made[0] += 1
                pool.wait_ge(pool_own, made[0])

            own(pool.memset(ident[:, :], 0.0))
            pool.affine_select(out=ident[:, :], in_=ident[:, :], compare_op=ALU.not_equal, fill=1.0, base=0,
                               pattern=[[-1, P]], channel_multiplier=1).then_inc(ident_ok, 1)
            own(pool.memset(head8[:, :], 1.0))
            for sign in (1, -1):
                own(pool.affine_select(out=head8[:, :], in_=head8[:, :], compare_op=ALU.is_ge, fill=0.0,
                                       base=0 if sign > 0 else DH - 1, pattern=[[-sign * DH, H]],
                                       channel_multiplier=sign))
            own(pool.memset(head16[:, :], 1.0))
            for sign in (1, -1):
                own(pool.affine_select(out=head16[:, :], in_=head16[:, :], compare_op=ALU.is_ge, fill=0.0,
                                       base=0 if sign > 0 else S - 1, pattern=[[-sign * S, P // S]],
                                       channel_multiplier=sign))
            own(pool.memset(sel3[:, :, :], 0.0))
            own(pool.affine_select(out=sel3[:, :, :], in_=sel3[:, :, :], compare_op=ALU.not_equal, fill=1.0,
                                   base=0, pattern=[[-S, P // S], [-1, S]], channel_multiplier=1))
            own(pool.memset(repS[:, :, :], 0.0))
            each = repS[:, :, :].rearrange("p g (j b) -> p (g j) b", b=Q)
            own(pool.affine_select(out=each, in_=each, compare_op=ALU.not_equal, fill=1.0,
                                   base=0, pattern=[[-1, S], [0, Q]], channel_multiplier=1))
            own(pool.memset(epsT[:, :], EPS))
            own(pool.memset(mhalf[:, :], -0.5))
            own(pool.memset(aoT[:, :, :], 0.0))
            own(pool.memset(hT[:, :, :], 0.0))
            own(pool.memset(pvm[:, :, :, :], 0.0))
            own(pool.memset(xn[:, :, :, :], 1.0))
            own(pool.memset(xn2[:, :, :, :], 1.0))
            pool.sem_inc(masks_ok, 1)

            def step(half, par):
                if live(half, par, 4):
                    b, k, n = turn(half, par, 4)
                    wait(pool, mv2_ok, b + 1)
                    pool.tensor_tensor(ve2[:, k, :], mv2[:, k, :, 1], epsT[:, 0:2], ALU.add).then_inc(ve2_ok, 1)
                    wait(pool, ve2_ok, b + 1)
                    pool.tensor_tensor(rs2[:, k, :], ve2[:, k, :], mhalf[:, 0:2], ALU.pow).then_inc(rs2_ok, 1)
                if live(half, par, 2):
                    b, k, n = turn(half, par, 2)
                    wait(pool, rz_ok, b + 1)
                    wait(pool, ft_ok, b + 1)
                    wait(pool, tq_ok, b - 1)
                    for j in range(2):
                        last = pool.tensor_tensor(heads(qz[:, k, j, :], DH), heads(ft[:, k, j, 0:P], DH),
                                                  over(rz[:, k, j * H:(j + 1) * H], DH), ALU.mult)
                    last.then_inc(qz_ok, 1)
                if live(half, par, 0):
                    b, k, n = turn(half, par, 0)
                    wait(pool, mv1_ok, b + 1)
                    pool.tensor_tensor(ve1[:, k, :], mv1[:, k, :, 1], epsT[:, 0:2], ALU.add).then_inc(ve1_ok, 1)
                    wait(pool, ve1_ok, b + 1)
                    pool.tensor_tensor(rs1[:, k, :], ve1[:, k, :], mhalf[:, 0:2], ALU.pow).then_inc(rs1_ok, 1)
                    wait(pool, xn_ok, b + 1)
                    pool.tensor_tensor(X[:, b, :].rearrange("p (j d) -> p j d", j=2),
                                       X[:, b, :].rearrange("p (j d) -> p j d", j=2),
                                       under(a_bo_all[:, :], 2), ALU.add).then_inc(xbo_ok, 1)
                if live(half, par, 4):
                    b, k, n = turn(half, par, 4)
                    wait(pool, xn2_ok, b + 1)
                    pool.tensor_tensor(X[:, b, :].rearrange("p (j d) -> p j d", j=2),
                                       X[:, b, :].rearrange("p (j d) -> p j d", j=2),
                                       under(c_bo_all[:, :], 2), ALU.add).then_inc(xcbo_ok, 1)

            for g in range(4):
                pool.wait_ge(x_in[g], 16)
            pool.wait_ge(w_in, 16 * N_SMALL)
            pipeline(pool, step, NB + LAGS1, FIRST1, NB)

            pool.wait_ge(mid_dve, 1 + G)
            pool.tensor_tensor(ve3[:, :], mv3[:, :, 1], epsT[:, :], ALU.add).then_inc(mid_pool, 1)
            pool.wait_ge(mid_pool, 1)
            pool.tensor_tensor(rs3[:, :], ve3[:, :], mhalf[:, :], ALU.pow).then_inc(mid_pool, 1)

            def step2(half, par):
                if live(half, par, 3):
                    b, k, n = turn(half, par, 3)
                    wait(pool, rsm_ok, b + 1)
                    wait(pool, tt_ok, b - 1)
                    for j in range(2):
                        last = pool.tensor_tensor(heads(at[:, k, j * HS:(j + 1) * HS], S),
                                                  heads(ep[:, k, j * HS:(j + 1) * HS], S),
                                                  over(rsm[:, k, j * H:(j + 1) * H], S), ALU.mult)
                    last.then_inc(at_ok, 1)
                if live(half, par, 0):
                    b, k, n = turn(half, par, 0)
                    wait(pool, ap_ok, b - 1)
                    pool.tensor_tensor(heads(BDk[:, k, :], S), under(kT[:, :, b], H), over(head8[:, :], S),
                                       ALU.mult).then_inc(bdk_ok, 1)
                if live(half, par, 2):
                    b, k, n = turn(half, par, 2)
                    wait(pool, vwp_ok, b - 1)
                    pool.tensor_tensor(heads(BDv[:, k, :], S), under(vT[:, :, b], H), over(head8[:, :], S),
                                       ALU.mult).then_inc(bdv_ok, 1)

            pool.wait_ge(kT_ok, 1)
            pool.wait_ge(vT_ok, 1)
            pipeline(pool, step2, NB + LAGS2, FIRST2, NB)

        @block.scalar
        def _(sc):
            for g in range(4):
                sc.dma_start(X[:, 4 * g:4 * g + 4, :], x_rows[:, 4 * g:4 * g + 4, :]).then_inc(x_in[g], 16)
            sc.wait_ge(su_pe, 2)
            sc.activation(Wt[:, :, :], ps[:, 5, 0:3 * P].rearrange("p (m n) -> p m n", m=3),
                          ACT.Copy).then_inc(su_act, 1)
            sc.wait_ge(su_pe, 3)
            sc.activation(Wproj[:, 0:2 * P], ps[:, 4, 0:2 * P], ACT.Copy, scale=0.25)
            sc.activation(WvP[:, :], ps[:, 4, 2 * P:3 * P], ACT.Copy)
            sc.activation(WoT[:, :], ps[:, 4, 3 * P:4 * P], ACT.Copy)
            sc.wait_ge(su_pe, 4)
            sc.activation(Wproj[:, 2 * P:4 * P], ps[:, 3, 0:2 * P], ACT.Copy, scale=SC)
            sc.wait_ge(su_pe, 6)
            sc.activation(dWvP[:, :], ps[:, 1, 0:P], ACT.Copy)
            sc.wait_ge(su_pe, 7)
            sc.activation(Ad[:, :], ps[:, 0, 0:HS], ACT.Copy).then_inc(su_act, 1)

            def step(half, par):
                if live(half, par, 2):
                    b, k, n = turn(half, par, 2)
                    wait(sc, ex_ok, b + 1)
                    wait(sc, kv_ok, b - 1)
                    wait(sc, qz_ok, b - 1)
                    sc.activation(ft[:, k], ex[:, k], ACT.Exp).then_inc(ft_ok, 1)
                if live(half, par, 1):
                    b, k, n = turn(half, par, 1)
                    wait(sc, tx_ok, b + 1)
                    wait(sc, vp_ok, b - 1)
                    sc.activation(xnT[:, k, :], ps[:, 3, 0:NT], ACT.Copy).then_inc(xnT_ok, 1)
                if live(half, par, 3):
                    b, k, n = turn(half, par, 3)
                    wait(sc, tq_ok, b + 1)
                    wait(sc, out_ok, b - 1)
                    sc.activation(Mb[:, k, :], ps[:, 5, NT:NT + P], ACT.Copy).then_inc(mb_ok, 1)
                    sc.activation(qzT[:, k, :], ps[:, 5, 0:NT], ACT.Copy).then_inc(qzT_ok, 1)
                if live(half, par, 5):
                    b, k, n = turn(half, par, 5)
                    wait(sc, nmax_ok, b + 1)
                    wait(sc, tp_ok, b - 1)
                    wait(sc, rps_ok, b - 1)
                    for hf in range(2):
                        last = sc.activation(pr[:, k, hf, :], ps[:, 4, hf * NT:(hf + 1) * NT], ACT.Exp,
                                             bias=nmax[:, k, hf:hf + 1], accum_out=psm[:, k, hf:hf + 1])
                    last.then_inc(pr_ok, 1)
                if live(half, par, 1):
                    b, k, n = turn(half, par, 1)
                    wait(sc, proj_ok, b + 1)
                    wait(sc, ss_ok, b - 1)
                    sc.activation(sq[:, k], ps[:, 0:2, 0:2 * P], ACT.Square).then_inc(sq_ok, 1)
                    wait(sc, vp_ok, b + 1)
                    wait(sc, kv_ok, b - 1)
                    sc.activation(Vs[:, k], ps[:, 2, 0:2 * P].rearrange("p (j d) -> p j d", j=2),
                                  ACT.Copy).then_inc(v_ok, 1)
                if live(half, par, 4):
                    b, k, n = turn(half, par, 4)
                    wait(sc, tx2_ok, b + 1)
                    wait(sc, v2p_ok, b - 1)
                    wait(sc, saved[k], n * 16, NB * 8)
                    sc.activation(xn2T[:, k, :], ps[:, 3, 0:NT], ACT.Copy).then_inc(xn2T_ok, 1)
                if live(half, par, 5):
                    b, k, n = turn(half, par, 5)
                    wait(sc, tp_ok, b + 1)
                    wait(sc, pv_ok, b - 1)
                    sc.activation(prT[:, k], ps[:, 5, :].rearrange("p (j m) -> p j m", j=2),
                                  ACT.Copy).then_inc(prT_ok, 1)
                if live(half, par, 4):
                    b, k, n = turn(half, par, 4)
                    wait(sc, v2p_ok, b + 1)
                    wait(sc, pv_ok, b - 1)
                    sc.activation(V2s[:, k], ps[:, 2, 0:2 * P].rearrange("p (j d) -> p j d", j=2),
                                  ACT.Copy).then_inc(v2_ok, 1)

            pipeline(sc, step, NB + LAGS1, FIRST1, NB)

            def act_columns(g):
                sc.wait_ge(ta_ok, g + 1)
                if g >= 2:
                    sc.wait_ge(y_ok, g - 1)
                sc.activation(actT[:, g % 2], ps[:, 1, :].rearrange("p (c m) -> p c m", c=FC),
                              ACT.Copy).then_inc(actT_ok, 1)

            for g in range(G):
                bank = 2 + 2 * (g % 3)
                sc.wait_ge(up_ok, g + 1)
                if g >= 2:
                    sc.wait_ge(sg_ok, g - 1)
                sc.activation(th[g % 2], ps[:, bank:bank + 2, :], ACT.Tanh, scale=0.5).then_inc(th_ok, 1)
                if g >= 1:
                    act_columns(g - 1)
            act_columns(G - 1)

            def step2(half, par):
                if live(half, par, 4):
                    b, k, n = turn(half, par, 4)
                    wait(sc, tt_ok, b + 1)
                    wait(sc, op_ok, b - 1)
                    sc.activation(atT[:, k], ps[:, 4 + k, :].rearrange("p (h t) -> p h t", h=2),
                                  ACT.Copy).then_inc(atT_ok, 1)
                if live(half, par, 1):
                    b, k, n = turn(half, par, 1)
                    wait(sc, ap_ok, b + 1)
                    wait(sc, sp_ok, b - 1)
                    sc.activation(As[:, k, :], ps[:, k, 0:HS], ACT.Copy).then_inc(a_ok, 1)
                if live(half, par, 3):
                    b, k, n = turn(half, par, 3)
                    wait(sc, vwp_ok, b + 1)
                    wait(sc, op_ok, b - 1)
                    sc.activation(VWs[:, k, :], ps[:, 1 - k, 0:HS], ACT.Copy).then_inc(vw_ok, 1)
                if live(half, par, 2):
                    b, k, n = turn(half, par, 2)
                    wait(sc, sx_ok, b + 1)
                    wait(sc, at_ok, b - 1)
                    wait(sc, sm_ok, b - 1)
                    sc.activation(ep[:, k, :], sx[:, k, :], ACT.Exp).then_inc(ep_ok, 1)

            pipeline(sc, step2, NB + LAGS2, FIRST2, NB)

        @block.vector
        def _(ve):
            ve.wait_ge(masks_ok, 1)
            ve.wait_ge(w_in, 16 * N_SMALL)
            ve.tensor_reduce(selS[:, :], sel3[:, :, :].rearrange("p h s -> p s h"), AX.X, ALU.add)
            ve.tensor_tensor(heads(BDR[:, :], DH), under(Rrep[:, :], H), over(head8[:, :], DH), ALU.mult)
            for m in (AQ, AK, AV):
                ve.tensor_scalar(W[:, m, 0:L], W[:, m, 0:L], W[:, m, L:P], None, ALU.subtract)
            ve.tensor_tensor(slotb[:, :], vec[SLOT:SLOT + S, :], d_bo_all[:, :], ALU.add).then_inc(su_dve, 1)
            ve.wait_ge(su_pe, 1)
            ve.tensor_copy(vecT[:, :], ps[:, 7, 0:NR]).then_inc(su_dve, 1)
            ve.wait_ge(su_dve, 2)
            ve.tensor_copy(W[:, AQ:AV + 1, L], vecT[:, BQ:BV + 1]).then_inc(su_dve, 1)
            ve.wait_ge(su_act, 1)
            for m in range(3):
                last = ve.tensor_scalar(Wt[:, m, 0:L], Wt[:, m, 0:L], Wt[:, m, L:P], None, ALU.subtract)
            last.then_inc(passed, 1)
            ve.wait_ge(passed, 1)
            ve.tensor_copy(Wt[:, :, L], vecT[:, BDK:BCQ + 1])
            ve.wait_ge(su_pe, 5)
            ve.tensor_scalar(qTs[:, :], ps[:, 2, 0:S], vecT[:, BDQ:BDQ + 1], SC, ALU.add,
                             ALU.mult).then_inc(passed, 1)
            ve.wait_ge(passed, 2)
            ve.tensor_tensor(heads(qbd[:, :], S), under(qTs[:, :], H), over(head8[:, :], S),
                             ALU.mult).then_inc(su_dve, 1)
            for g in range(4):
                ve.wait_ge(x_in[g], 16)
            ve.wait_ge(su_act, 2)

            def step(half, par):
                if live(half, par, 6):
                    b, k, n = turn(half, par, 6)
                    wait(ve, pr_ok, b + 1)
                    ve.reciprocal(rps[:, k, :], psm[:, k, :]).then_inc(rps_ok, 1)
                    wait(ve, rps_ok, b + 1)
                    wait(ve, pv_ok, b + 1)
                    wait(ve, sel_ok, b - 1)
                    for hf in range(2):
                        last = ve.scalar_tensor_tensor(
                            out=heads(pvm[:, k, hf, hf * 64:hf * 64 + 64], DH),
                            in0=heads(ps[:, 7, hf * 64:hf * 64 + 64], DH),
                            scalar=rps[:, k, hf:hf + 1], in1=over(head16[:, :], DH), op0=ALU.mult, op1=ALU.mult)
                    last.then_inc(pvm_ok, 1)
                if live(half, par, 5):
                    b, k, n = turn(half, par, 5)
                    wait(ve, s_ok, b + 1)
                    ve.tensor_reduce(nmax[:, k, :], ps[:, 4, :].rearrange("p (h t) -> p h t", h=2), AX.X,
                                     ALU.max, negate=True).then_inc(nmax_ok, 1)
                if live(half, par, 4):
                    b, k, n = turn(half, par, 4)
                    wait(ve, rs2_ok, b + 1)
                    wait(ve, tx2_ok, b - 1)
                    for j in range(2):
                        last = ve.tensor_scalar(xn2[:, k, j, 0:L], X[:, b, j * P:j * P + L], mv2[:, k, j, 0:1],
                                                rs2[:, k, j:j + 1], ALU.subtract, ALU.mult)
                    last.then_inc(xn2_ok, 1)
                if live(half, par, 2):
                    b, k, n = turn(half, par, 2)
                    wait(ve, ft_ok, b + 1)
                    ve.tensor_reduce(den[:, k, :].rearrange("p (j h) -> p j h", j=2),
                                     ft[:, k, :, 0:P].rearrange("p j (h d) -> p j h d", d=DH), AX.X,
                                     ALU.add).then_inc(den_ok, 1)
                if live(half, par, 2):
                    b, k, n = turn(half, par, 2)
                    wait(ve, den_ok, b + 1)
                    ve.tensor_scalar(den2[:, k, :], den[:, k, :], 1e-8, None, ALU.add).then_inc(den2_ok, 1)
                    wait(ve, den2_ok, b + 1)
                    wait(ve, qz_ok, b - 1)
                    ve.reciprocal(rz[:, k, :], den2[:, k, :]).then_inc(rz_ok, 1)
                    wait(ve, kv_ok, b + 1)
                    wait(ve, tq_ok, b - 1)
                    ve.tensor_tensor(heads(kvm[:, k, :], DH), heads(ps[:, 6, NT:NT + P], DH), over(head8[:, :], DH),
                                     ALU.mult).then_inc(kvm_ok, 1)
                if live(half, par, 6):
                    b, k, n = turn(half, par, 6)
                    wait(ve, sel_ok, b + 1)
                    ve.tensor_scalar(aoT[:, :, b], ps[:, 7, P:P + S], 1.0, None,
                                     ALU.mult).then_inc(ao_ok, 1)
                if live(half, par, 0):
                    b, k, n = turn(half, par, 0)
                    for j in range(2):
                        last = ve.bn_stats(st1[:, k, j, :], X[:, b, j * P:(j + 1) * P])
                    last.then_inc(bn1_ok, 1)
                if live(half, par, 0):
                    b, k, n = turn(half, par, 0)
                    wait(ve, bn1_ok, b + 1)
                    wait(ve, rs1_ok, b - 1)
                    ve.sem_inc(dve_carry, 1)
                    for j in range(2):
                        last = ve.bn_aggr(mv1[:, k, j, :], st1[:, k, j, :])
                    last.then_inc(mv1_ok, 1)
                if live(half, par, 1):
                    b, k, n = turn(half, par, 1)
                    wait(ve, sq_ok, b + 1)
                    ve.tensor_reduce(ss[:, k, :].rearrange("p (j h) -> p j h", j=2),
                                     sq[:, k].rearrange("p j (h d) -> p j h d", d=DH), AX.X,
                                     ALU.add).then_inc(ss_ok, 1)
                    wait(ve, ss_ok, b + 1)
                    wait(ve, ft_ok, b - 1)
                    ve.tensor_tensor(ex[:, k].rearrange("p j (h d) -> p j h d", d=DH),
                                     ps[:, 0:2, 2 * P:4 * P].rearrange("p j (h d) -> p j h d", d=DH),
                                     ss[:, k, :].rearrange("p (j h) -> p j h", j=2).unsqueeze(3)
                                     .broadcast_to([P, 2, 2 * H, DH]), ALU.subtract).then_inc(ex_ok, 1)
                if live(half, par, 3):
                    b, k, n = turn(half, par, 3)
                    wait(ve, out_ok, b + 1)
                    wait(ve, xbo_ok, b + 1)
                    ve.tensor_tensor(X[:, b, :], ps[:, 6, 0:NT], X[:, b, :], ALU.add).then_inc(x2_ok, 1)
                if live(half, par, 3):
                    b, k, n = turn(half, par, 3)
                    wait(ve, x2_ok, b + 1)
                    ve.sem_inc(dve_carry, 1)
                    for j in range(2):
                        last = ve.bn_stats(st2[:, k, j, :], X[:, b, j * P:(j + 1) * P])
                    last.then_inc(bn2_ok, 1)
                if live(half, par, 0):
                    b, k, n = turn(half, par, 0)
                    wait(ve, rs1_ok, b + 1)
                    wait(ve, tx_ok, b - 1)
                    for j in range(2):
                        last = ve.tensor_scalar(xn[:, k, j, 0:L], X[:, b, j * P:j * P + L], mv1[:, k, j, 0:1],
                                                rs1[:, k, j:j + 1], ALU.subtract, ALU.mult)
                    last.then_inc(xn_ok, 1)
                if live(half, par, 3):
                    b, k, n = turn(half, par, 3)
                    wait(ve, bn2_ok, b + 1)
                    ve.sem_inc(dve_carry, 1)
                    for j in range(2):
                        last = ve.bn_aggr(mv2[:, k, j, :], st2[:, k, j, :])
                    last.then_inc(mv2_ok, 1)

            pipeline(ve, step, NB + LAGS1, FIRST1, NB)

            ve.wait_ge(mid_pe, 1)
            for g in range(G):
                last = ve.bn_stats(st3[:, g, :], ps[:, 0, g * P:(g + 1) * P])
            last.then_inc(mid_dve, 1)
            ve.wait_ge(mid_dve, 1)
            for g in range(G):
                ve.bn_aggr(mv3[:, g, :], st3[:, g, :]).then_inc(mid_dve, 1)
            ve.wait_ge(mid_pool, 2)
            for g in range(G):
                last = ve.tensor_scalar(xh[:, g, :], ps[:, 0, g * P:(g + 1) * P], mv3[:, g, 0:1], rs3[:, g:g + 1],
                                        ALU.subtract, ALU.mult)
            last.then_inc(mid_dve, 1)
            ve.wait_ge(mid_pe, 2)
            ve.tensor_tensor(hg[:, :, :], ps[:, 1, :].rearrange("p (s b) -> p s b", b=Q)[:, :, 0:NB],
                             over(vecT[:, GAIN:GAIN + S], NB), ALU.mult).then_inc(mid_dve, 1)
            ve.wait_ge(mid_dve, G + 3)
            ve.tensor_tensor(hT[:, :, 0:NB], hg[:, :, :], over(vecT[:, SHIFT:SHIFT + S], NB),
                             ALU.add).then_inc(mid_dve, 1)

            for g in range(G):
                bank = 2 + 2 * (g % 3)
                ve.wait_ge(th_ok, g + 1)
                for u in range(2):
                    last = ve.scalar_tensor_tensor(out=sg[g % 2][:, u, :], in0=th[g % 2][:, u, :], scalar=1.0,
                                                   in1=ps[:, bank + u, :], op0=ALU.add, op1=ALU.mult)
                last.then_inc(sg_ok, 1)
                ve.wait_ge(sg_ok, g + 1)
                if g >= 2:
                    ve.wait_ge(ta_ok, g - 1)
                ve.scalar_tensor_tensor(out=act[:, g % 2], in0=sg[g % 2][:, 0, :], scalar=0.25,
                                        in1=sg[g % 2][:, 1, :], op0=ALU.mult, op1=ALU.mult).then_inc(act_ok, 1)
            ve.wait_ge(y_ok, G)
            ve.tensor_copy(o2[:, :, :], ps[:, 0, :].rearrange("p (g d) -> p g d", g=G)).then_inc(o2s_ok, 1)
            ve.wait_ge(to_ok, 1)
            ve.tensor_tensor(o2T[:, :].rearrange("p (s b) -> p s b", b=NB),
                             ps[:, 1, :].rearrange("p (s b) -> p s b", b=Q)[:, :, 0:NB],
                             over(vecT[:, B2:B2 + S], NB), ALU.add).then_inc(o2_ok, 1)
            ve.wait_ge(kvp_ok, 1)
            ve.tensor_scalar(kT[:, :, :].rearrange("p s b -> p (s b)"), ps[:, 6, 0:2 * P],
                             vecT[:, BCK:BCK + 1], SC, ALU.add, ALU.mult).then_inc(kT_ok, 1)
            ve.wait_ge(kvp_ok, 2)
            ve.tensor_scalar(vT[:, :, :].rearrange("p s b -> p (s b)"), ps[:, 7, 0:2 * P],
                             vecT[:, BCV:BCV + 1], None, ALU.add).then_inc(vT_ok, 1)

            def step2(half, par):
                if live(half, par, 3):
                    b, k, n = turn(half, par, 3)
                    wait(ve, ep_ok, b + 1)
                    ve.tensor_reduce(sm[:, k, :], heads(ep[:, k, :], S), AX.X, ALU.add).then_inc(sm_ok, 1)
                    wait(ve, sm_ok, b + 1)
                    wait(ve, at_ok, b - 1)
                    ve.reciprocal(rsm[:, k, :], sm[:, k, :]).then_inc(rsm_ok, 1)
                if live(half, par, 2):
                    b, k, n = turn(half, par, 2)
                    wait(ve, sp_ok, b + 1)
                    ve.tensor_reduce(mx[:, k, :], heads(ps[:, 2 + k, :], S), AX.X, ALU.max).then_inc(mx_ok, 1)
                    wait(ve, mx_ok, b + 1)
                    wait(ve, ep_ok, b - 1)
                    ve.tensor_tensor(heads(sx[:, k, :], S), heads(ps[:, 2 + k, :], S), over(mx[:, k, :], S),
                                     ALU.subtract).then_inc(sx_ok, 1)
                if live(half, par, 4):
                    b, k, n = turn(half, par, 4)
                    wait(ve, op_ok, b + 1)
                    wait(ve, stored[k], n * 16, NB * 8)
                    ve.tensor_tensor(ob[:, k, :], ps[:, 6 + k, 0:NT], X[:, b, :], ALU.add).then_inc(ob_ok, 1)

            ve.wait_ge(xcbo_ok, NB)
            pipeline(ve, step2, NB + LAGS2, FIRST2, NB)

        @block.tensor
        def _(pe):
            pe.wait_ge(ident_ok, 1)
            pe.wait_ge(w_in, 16 * N_SMALL)
            pe.transpose(ps[:, 7, 0:NR], vec[:, :], ident[0:NR, 0:NR]).then_inc(su_pe, 1)
            for n, m in enumerate((DK, DV, CQ)):
                last = pe.transpose(ps[:, 5, n * P:(n + 1) * P], W[:, m, :], ident[:, :])
            last.then_inc(su_pe, 1)
            pe.wait_ge(su_dve, 3)
            for n, m in enumerate((AQ, AK, AV, AO)):
                last = pe.transpose(ps[:, 4, n * P:(n + 1) * P], W[:, m, :], ident[:, :])
            last.then_inc(su_pe, 1)
            for n, m in enumerate((AQ, AK)):
                last = pe.matmul(ps[:, 3, n * P:(n + 1) * P], W[:, m, :], BDR[:, :], start=True, stop=True)
            last.then_inc(su_pe, 1)
            pe.matmul(ps[:, 2, 0:S], W[:, DQ, :], vecT[:, SLOT:SLOT + S], start=True,
                      stop=True).then_inc(su_pe, 1)
            pe.wait_ge(su_dve, 4)
            pe.transpose(ps[:, 1, 0:P], Wt[:, 1, :], ident[:, :]).then_inc(su_pe, 1)
            pe.matmul(ps[:, 0, 0:HS], Wt[:, 0, :], qbd[:, :], start=True, stop=True).then_inc(su_pe, 1)
            pe.wait_ge(su_act, 2)

            def step(half, par):
                if live(half, par, 3):
                    b, k, n = turn(half, par, 3)
                    wait(pe, kvm_ok, b + 1)
                    wait(pe, qzT_ok, b)
                    wait(pe, prT_ok, b - 2)
                    pe.matmul(ps[:, 5, NT:NT + P], kvm[:, k, :], WoT[:, :], start=True, stop=True)
                if live(half, par, 1):
                    b, k, n = turn(half, par, 1)
                    wait(pe, xn_ok, b + 1)
                    wait(pe, xnT_ok, b)
                    wait(pe, xn2T_ok, b - 3)
                    for j in range(2):
                        last = pe.transpose(ps[:, 3, j * P:(j + 1) * P], xn[:, k, j, :], ident[:, :])
                    last.then_inc(tx_ok, 1)
                if live(half, par, 3):
                    b, k, n = turn(half, par, 3)
                    wait(pe, qz_ok, b + 1)
                    for j in range(2):
                        last = pe.transpose(ps[:, 5, j * P:(j + 1) * P], qz[:, k, j, :], ident[:, :])
                    last.then_inc(tq_ok, 1)
                if live(half, par, 2):
                    b, k, n = turn(half, par, 2)
                    wait(pe, ft_ok, b + 1)
                    wait(pe, v_ok, b + 1)
                    wait(pe, kvm_ok, b)
                    wait(pe, x2_ok, b - 1)
                    for j in range(2):
                        last = pe.matmul(ps[:, 6, NT:NT + P], Vs[:, k, j, :], ft[:, k, j, P:2 * P], start=(j == 0),
                                         stop=(j == 1))
                    last.then_inc(kv_ok, 1)
                if live(half, par, 6):
                    b, k, n = turn(half, par, 6)
                    wait(pe, pvm_ok, b + 1)
                    for hf in range(2):
                        last = pe.matmul(ps[:, 7, P:P + S], pvm[:, k, hf, :], selS[:, :],
                                         start=(hf == 0), stop=(hf == 1))
                    last.then_inc(sel_ok, 1)
                if live(half, par, 1):
                    b, k, n = turn(half, par, 1)
                    wait(pe, xnT_ok, b + 1)
                    wait(pe, ex_ok, b)
                    for j in range(2):
                        last = pe.matmul(ps[:, j, :], xnT[:, k, j * P:(j + 1) * P], Wproj[:, :], start=True,
                                         stop=True)
                    last.then_inc(proj_ok, 1)
                    wait(pe, v_ok, b)
                    wait(pe, v2_ok, b - 3)
                    for j in range(2):
                        last = pe.matmul(ps[:, 2, j * P:(j + 1) * P], xnT[:, k, j * P:(j + 1) * P], WvP[:, :],
                                         start=True, stop=True)
                    last.then_inc(vp_ok, 1)
                if live(half, par, 4):
                    b, k, n = turn(half, par, 4)
                    wait(pe, xn2_ok, b + 1)
                    wait(pe, xnT_ok, b + 4)
                    wait(pe, xn2T_ok, b)
                    for j in range(2):
                        last = pe.transpose(ps[:, 3, j * P:(j + 1) * P], xn2[:, k, j, :], ident[:, :])
                    last.then_inc(tx2_ok, 1)
                if live(half, par, 5):
                    b, k, n = turn(half, par, 5)
                    wait(pe, pr_ok, b + 1)
                    wait(pe, qzT_ok, b + 3)
                    wait(pe, prT_ok, b)
                    for j in range(2):
                        for hf in range(2):
                            last = pe.transpose(ps[:, 5, j * HS + hf * P:j * HS + (hf + 1) * P],
                                                pr[:, k, hf, j * P:(j + 1) * P], ident[:, :])
                    last.then_inc(tp_ok, 1)
                if live(half, par, 3):
                    b, k, n = turn(half, par, 3)
                    wait(pe, mb_ok, b + 1)
                    wait(pe, qzT_ok, b + 1)
                    wait(pe, kvm_ok, b + 2)
                    wait(pe, x2_ok, b)
                    for j in range(2):
                        last = pe.matmul(ps[:, 6, j * P:(j + 1) * P], qzT[:, k, j * P:(j + 1) * P], Mb[:, k, :],
                                         start=True, stop=True)
                    last.then_inc(out_ok, 1)
                if live(half, par, 4):
                    b, k, n = turn(half, par, 4)
                    wait(pe, xn2T_ok, b + 1)
                    wait(pe, pr_ok, b)
                    for hf in range(2):
                        last = pe.matmul(ps[:, 4, hf * NT:(hf + 1) * NT], Ad[:, hf * P:(hf + 1) * P],
                                         xn2T[:, k, :], start=True, stop=True)
                    last.then_inc(s_ok, 1)
                    wait(pe, v_ok, b + 4)
                    wait(pe, v2_ok, b)
                    for j in range(2):
                        last = pe.matmul(ps[:, 2, j * P:(j + 1) * P], xn2T[:, k, j * P:(j + 1) * P], dWvP[:, :],
                                         start=True, stop=True)
                    last.then_inc(v2p_ok, 1)
                if live(half, par, 5):
                    b, k, n = turn(half, par, 5)
                    wait(pe, prT_ok, b + 1)
                    wait(pe, v2_ok, b + 1)
                    wait(pe, ao_ok, b)
                    for hf in range(2):
                        for j in range(2):
                            last = pe.matmul(ps[:, 7, hf * 64:hf * 64 + 64], prT[:, k, j, hf * P:(hf + 1) * P],
                                             V2s[:, k, j, hf * 64:hf * 64 + 64], start=(j == 0), stop=(j == 1))
                    last.then_inc(pv_ok, 1)

            pipeline(pe, step, NB + LAGS1, FIRST1, NB)

            for g in range(G):
                pe.matmul(ps[:, 0, g * P:(g + 1) * P], repS[:, g, :], slotb[:, :], start=(g == 0), stop=False,
                          skip_group_check=True)
            pe.wait_ge(ao_ok, NB)
            for g in range(G):
                last = pe.matmul(ps[:, 0, g * P:(g + 1) * P],
                                 aoT[:, g * EG:(g + 1) * EG, :].rearrange("p s b -> p (s b)"), W[:, DO, :],
                                 start=False, stop=False, skip_group_check=True)
            last.then_inc(mid_pe, 1)

            def hidden_bias(g):
                for u in range(2):
                    pe.matmul(ps[:, 2 + 2 * (g % 3) + u, :], repS[:, g, :], fvec[:, u, :], start=True, stop=False,
                              skip_group_check=True)

            def experts_in(g):
                for u, w in enumerate((W1s, Wgs)):
                    for j in range(EG):
                        last = pe.matmul(ps[j * Q:(j + 1) * Q, 2 + 2 * (g % 3) + u, :], hT[:, g * EG + j, :],
                                         w[:, g * EG + j, :], start=False, stop=True, skip_group_check=True)
                last.then_inc(up_ok, 1)

            def experts_out(g):
                pe.wait_ge(act_ok, g + 1)
                if g >= 1:
                    pe.wait_ge(actT_ok, g)
                for c in range(FC):
                    last = pe.transpose(ps[:, 1, c * P:(c + 1) * P], act[:, g % 2, c * P:(c + 1) * P], ident[:, :])
                last.then_inc(ta_ok, 1)
                pe.wait_ge(actT_ok, g + 1)
                for c in range(FC):
                    for j in range(EG):
                        last = pe.matmul(ps[j * Q:(j + 1) * Q, 0, g * P:(g + 1) * P],
                                         actT[:, g % 2, c, j * Q:(j + 1) * Q], W2s[:, g * EG + j, c, :],
                                         start=False, stop=(c == FC - 1), skip_group_check=True)
                last.then_inc(y_ok, 1)

            for g in range(3):
                hidden_bias(g)
            pe.wait_ge(mid_dve, G + 2)
            for g in range(G):
                last = pe.transpose(ps[:, 1, g * P:(g + 1) * P], xh[:, g, :], ident[:, :])
            last.then_inc(mid_pe, 1)
            pe.wait_ge(mid_dve, G + 4)
            pe.wait_ge(e_in, 16 * (8 + S))
            for g in range(G):
                if g == 3:
                    pe.wait_ge(sg_ok, 1)
                    hidden_bias(3)
                experts_in(g)
                if g >= 1:
                    experts_out(g - 1)
            experts_out(G - 1)
            pe.wait_ge(o2s_ok, 1)
            for g in range(G):
                last = pe.transpose(ps[:, 1, g * P:(g + 1) * P], o2[:, g, :], ident[:, :])
            last.then_inc(to_ok, 1)
            pe.wait_ge(o2_ok, 1)
            pe.matmul(ps[:, 6, 0:2 * P], W[:, CK, :], o2T[:, :], start=True, stop=True).then_inc(kvp_ok, 1)
            pe.matmul(ps[:, 7, 0:2 * P], W[:, CV, :], o2T[:, :], start=True, stop=True).then_inc(kvp_ok, 1)

            def step2(half, par):
                if live(half, par, 2):
                    b, k, n = turn(half, par, 2)
                    wait(pe, a_ok, b + 1)
                    wait(pe, xs_in[k], (n + 1) * 16, NB * 8)
                    wait(pe, sx_ok, b - 1)
                    for j in range(2):
                        last = pe.matmul(ps[:, 2 + k, j * HS:(j + 1) * HS], xs[:, k, j * P:(j + 1) * P],
                                         As[:, k, :], start=True, stop=True)
                    last.then_inc(sp_ok, 1)
                if live(half, par, 1):
                    b, k, n = turn(half, par, 1)
                    wait(pe, bdk_ok, b + 1)
                    wait(pe, a_ok, b - 1)
                    wait(pe, vw_ok, b - 2)
                    pe.matmul(ps[:, k, 0:HS], Wt[:, 2, :], BDk[:, k, :], start=True, stop=True).then_inc(ap_ok, 1)
                if live(half, par, 3):
                    b, k, n = turn(half, par, 3)
                    wait(pe, bdv_ok, b + 1)
                    wait(pe, a_ok, b + 2)
                    wait(pe, vw_ok, b - 1)
                    for hf in range(2):
                        last = pe.matmul(ps[:, 1 - k, hf * P:(hf + 1) * P], BDv[:, k, hf * P:(hf + 1) * P],
                                         W[:, CO, :], start=True, stop=True)
                    last.then_inc(vwp_ok, 1)
                if live(half, par, 4):
                    b, k, n = turn(half, par, 4)
                    wait(pe, atT_ok, b + 1)
                    wait(pe, ob_ok, b - 1)
                    for j in range(2):
                        for hf in range(2):
                            last = pe.matmul(ps[:, 6 + k, j * P:(j + 1) * P], atT[:, k, hf, j * P:(j + 1) * P],
                                             VWs[:, k, hf * P:(hf + 1) * P], start=(hf == 0),
                                             stop=(hf == 1))
                    last.then_inc(op_ok, 1)
                if live(half, par, 3):
                    b, k, n = turn(half, par, 3)
                    wait(pe, at_ok, b + 1)
                    wait(pe, atT_ok, b - 1)
                    for j in range(2):
                        for hf in range(2):
                            last = pe.transpose(ps[:, 4 + k, hf * NT + j * P:hf * NT + (j + 1) * P],
                                                at[:, k, j * HS + hf * P:j * HS + (hf + 1) * P], ident[:, :])
                    last.then_inc(tt_ok, 1)

            pipeline(pe, step2, NB + LAGS2, FIRST2, NB)


_INS = ['L0_attn_x', 'L0_attn_Wq', 'L0_attn_bq', 'L0_attn_Wk', 'L0_attn_bk', 'L0_attn_Wv', 'L0_attn_bv',
        'L0_attn_Wo', 'L0_attn_bo', 'L0_attn_R', 'L0_ffn_slot_query', 'L0_ffn_d_Wq', 'L0_ffn_d_Wk', 'L0_ffn_d_Wv',
        'L0_ffn_d_Wo', 'L0_ffn_d_bq', 'L0_ffn_d_bk', 'L0_ffn_d_bv', 'L0_ffn_d_bo', 'L0_ffn_c_Wq', 'L0_ffn_c_Wk',
        'L0_ffn_c_Wv', 'L0_ffn_c_Wo', 'L0_ffn_c_bq', 'L0_ffn_c_bk', 'L0_ffn_c_bv', 'L0_ffn_c_bo', 'L0_ffn_e_ln_g',
        'L0_ffn_e_ln_b', 'L0_ffn_e_W1', 'L0_ffn_e_b1', 'L0_ffn_e_Wg', 'L0_ffn_e_bg', 'L0_ffn_e_W2', 'L0_ffn_e_b2']
_OUTS = [((16, 256, 128), 'float32')]


def kernel(**inputs):
    import numpy as _np
    import concourse.bacc as _bacc
    from concourse import mybir as _mybir
    from concourse.bass_utils import run_bass_kernel_spmd as _run

    nc = _bacc.Bacc("TRN2", target_bir_lowering=False, num_devices=1)
    arrays, args = {}, []
    for name in _INS:
        a = _np.ascontiguousarray(inputs[name])
        arrays[f"in_{name}_dram"] = a
        args.append(nc.dram_tensor(f"in_{name}_dram", a.shape, _mybir.dt.from_np(a.dtype), kind="ExternalInput").ap())
    for i, (shape, dtype) in enumerate(_OUTS):
        dt = _mybir.dt.from_np(_np.dtype(dtype))
        args.append(nc.dram_tensor(f"out_{i}_dram", shape, dt, kind="ExternalOutput").ap())
    build(nc, *args)
    r = _run(nc, [arrays], core_ids=[0])
    got = tuple(r.results[0][f"out_{i}_dram"] for i in range(len(_OUTS)))
    return got[0]
```

```python
from contextlib import ExitStack

import numpy as np
import concourse.bass as bass
from concourse import mybir

F32 = mybir.dt.float32
BF16 = mybir.dt.bfloat16
ACT = mybir.ActivationFunctionType
ALU = mybir.AluOpType
AX = mybir.AxisListType

P = 128
NB = 16
NT = 256
H = 16
DH = P // H
S = 16
HS = H * S
FC = 4
F = FC * P
EG = 4
G = S // EG
Q = P // EG
L = P - 1
EPS = 1e-5
SC = float(1.0 / np.sqrt(DH))

AQ, AK, AV, AO, DK, DV, CQ, DQ, DO, CK, CV, CO = range(12)
SLOT, GAIN, SHIFT, B2, BIAS = 0, 16, 32, 48, 64
BQ, BK, BV, BDK, BDV, BCQ, BDQ, BCK, BCV = range(BIAS, BIAS + 9)
NR = BIAS + 9


def turn(half, par, lag):
    return half * 2 + (par - lag), (par - lag) % 2, half + (par - lag) // 2


def live(half, par, lag):
    return not isinstance(half, int) or 0 <= 2 * half + par - lag < NB


def wait(eng, sem, n, most=NB):
    if isinstance(n, int):
        n = min(n, most)
        if n <= 0:
            return
    eng.wait_ge(sem, n)


def pipeline(eng, step, steps, first, last, before={}):
    for t in range(first + 1):
        if t in before:
            before[t]()
        if t < first:
            step(t // 2, t % 2)
    with eng.Fori(0, (last - first) // 2) as i:
        step(i + first // 2, 0)
        step(i + first // 2, 1)
    for t in range(last, steps):
        if t in before:
            before[t]()
        step(t // 2, t % 2)


LAGS1, FIRST1 = 6, 8
LAGS2, FIRST2 = 7, 8


def build(nc, x, a_Wq, a_bq, a_Wk, a_bk, a_Wv, a_bv, a_Wo, a_bo, R, slot, d_Wq, d_Wk, d_Wv, d_Wo,
          d_bq, d_bk, d_bv, d_bo, c_Wq, c_Wk, c_Wv, c_Wo, c_bq, c_bk, c_bv, c_bo, ln_g, ln_b,
          W1, b1, Wg, bg, W2, b2, out):
    ctx = ExitStack()
    with ctx:
        def sb(name, *shape, dtype=F32):
            return ctx.enter_context(nc.sbuf_tensor(name, list(shape), dtype))

        def sem(name):
            return ctx.enter_context(nc.semaphore(name))

        X = sb("X", P, NB, NT)
        XN2T = sb("XN2T", P, NB, NT)
        W = sb("W", P, 12, P)
        W1s = sb("W1s", P, S, FC * P)
        Wgs = sb("Wgs", P, S, FC * P)
        W2s = sb("W2s", P, S, FC, P)
        vec = sb("vec", NR, P)
        vecT = sb("vecT", P, NR)
        fvec = W[0:3 * Q, 0:8, :].rearrange("p m d -> p (m d)")
        parts = sb("parts", 3 * Q, 2, 2 * F, dtype=BF16)
        a_bo_all = sb("a_bo_all", P, P)
        c_bo_all = sb("c_bo_all", P, P)
        d_bo_all = sb("d_bo_all", S, P)
        Rrep = sb("Rrep", P, DH)
        ident = sb("ident", P, P)
        head8 = sb("head8", P, H)
        head16 = sb("head16", P, P // S)
        sel3 = sb("sel3", P, P // S, S)
        selS = sb("selS", P, S)
        repS = sb("repS", S, G, P)
        rep3 = sb("rep3", 3 * Q, G, P, dtype=BF16)
        epsT = sb("epsT", P, G)
        mhalf = sb("mhalf", P, G)
        Wt = sb("Wt", P, 3, P)
        Wproj = sb("Wproj", P, 4 * P)
        WvP = sb("WvP", P, P)
        WoT = sb("WoT", P, P)
        BDR = sb("BDR", P, P)
        dWvP = sb("dWvP", P, P)
        qTs = sb("qTs", P, S)
        qbd = sb("qbd", P, HS)
        Ad = sb("Ad", P, HS)
        slotb = sb("slotb", S, P)
        st1 = sb("st1", P, 2, 2, 6)
        mv1 = sb("mv1", P, 2, 2, 2)
        ve1 = sb("ve1", P, 2, 2)
        rs1 = sb("rs1", P, 2, 2)
        xn = sb("xn", P, 2, 2, P)
        xnT = sb("xnT", P, 2, NT)
        sq = sb("sq", P, 2, 2, 2 * P)
        ss = sb("ss", P, 2, 4 * H)
        ex = sb("ex", P, 2, 2, 2 * P)
        ft = sb("ft", P, 2, 2, 2 * P)
        Vs = sb("Vs", P, 2, 2, P)
        den = sb("den", P, 2, 2 * H)
        den2 = sb("den2", P, 2, 2 * H)
        rz = sb("rz", P, 2, 2 * H)
        qz = sb("qz", P, 2, 2, P)
        qzT = sb("qzT", P, 2, NT)
        kvm = sb("kvm", P, 2, P)
        Mb = sb("Mb", P, 2, P)
        st2 = sb("st2", P, 2, 2, 6)
        mv2 = sb("mv2", P, 2, 2, 2)
        ve2 = sb("ve2", P, 2, 2)
        rs2 = sb("rs2", P, 2, 2)
        xn2 = sb("xn2", P, 2, 2, P)
        xn2T = sb("xn2T", P, 2, NT)
        nmax = sb("nmax", P, 2, 2)
        pr = sb("pr", P, 2, 2, NT)
        psm = sb("psm", P, 2, 2)
        rps = sb("rps", P, 2, 2)
        prT = sb("prT", P, 2, 2, HS)
        V2s = sb("V2s", P, 2, 2, P)
        pvm = sb("pvm", P, 2, P)
        aoT = sb("aoT", P, S, Q)
        st3 = sb("st3", P, G, 6)
        mv3 = sb("mv3", P, G, 2)
        ve3 = sb("ve3", P, G)
        rs3 = sb("rs3", P, G)
        xh = xn[:, :, :, :].rearrange("p k j d -> p (k j) d")
        hg = sb("hg", P, S, NB)
        hT = sb("hT", P, S, Q)
        flat3 = "p k j m -> p (k j m)"
        th = [t[:, :, :, :].rearrange(flat3).rearrange("p (u f) -> p u f", u=2) for t in (ft, ex)]
        sg = [t[:, :, :, :].rearrange(flat3).rearrange("p (u f) -> p u f", u=2) for t in (pr, sq)]
        act = sb("act", P, 2, F)
        actT = prT[:, :, :, :].rearrange("p k j m -> p k (j m)").rearrange("p k (c m) -> p k c m", c=FC)
        o2 = xn2[:, :, :, :].rearrange("p k j d -> p (k j) d")
        o2T = sb("o2T", P, S * NB)
        kT = sb("kT", P, S, NB)
        vT = sb("vT", P, S, NB)
        xs = xn2T
        BDk = xnT
        BDv = qzT
        flat = "p k j m -> p k (j m)"
        As = sq[:, :, 0, :]
        VWs = sq[:, :, 1, :]
        sx = ex[:, :, :, :].rearrange(flat)
        ep = ft[:, :, :, :].rearrange(flat)
        at = pr[:, :, :, :].rearrange(flat)
        atT = prT
        mx = sb("mx", P, 2, 2 * H)
        sm = sb("sm", P, 2, 2 * H)
        rsm = sb("rsm", P, 2, 2 * H)
        ob = V2s[:, :, :, :].rearrange(flat)

        ps = ctx.enter_context(nc.psum_tensor("ps", [P, 8, 512], F32))

        x_in = [sem(f"x_in{g}") for g in range(4)]
        w_attn, w_slots, w_rest, e_in = sem("w_attn"), sem("w_slots"), sem("w_rest"), sem("e_in")
        f_in, parts_act, parts_pool = sem("f_in"), sem("parts_act"), sem("parts_pool")
        pool_own, ident_ok, ones_ok, masks_ok = (sem(n) for n in ("pool_own", "ident_ok", "ones_ok", "masks_ok"))
        su_pe, su_act, su_dve = sem("su_pe"), sem("su_act"), sem("su_dve")
        bn1_ok, mv1_ok, ve1_ok, rs1_ok, xn_ok = (sem(n) for n in ("bn1_ok", "mv1_ok", "ve1_ok", "rs1_ok", "xn_ok"))
        xbo_ok = sem("xbo_ok")
        tx_ok, xnT_ok, proj_ok, vp_ok, v_ok = (sem(n) for n in ("tx_ok", "xnT_ok", "proj_ok", "vp_ok", "v_ok"))
        sq_ok, ss_ok, ex_ok, ft_ok = (sem(n) for n in ("sq_ok", "ss_ok", "ex_ok", "ft_ok"))
        den_ok, den2_ok, rz_ok, qz_ok = (sem(n) for n in ("den_ok", "den2_ok", "rz_ok", "qz_ok"))
        kv_ok, kvm_ok, mb_ok = (sem(n) for n in ("kv_ok", "kvm_ok", "mb_ok"))
        tq_ok, qzT_ok, out_ok, x2_ok = (sem(n) for n in ("tq_ok", "qzT_ok", "out_ok", "x2_ok"))
        bn2_ok, mv2_ok, ve2_ok, rs2_ok, xn2_ok = (sem(n) for n in ("bn2_ok", "mv2_ok", "ve2_ok", "rs2_ok", "xn2_ok"))
        tx2_ok, xn2T_ok, s_ok, nmax_ok = (sem(n) for n in ("tx2_ok", "xn2T_ok", "s_ok", "nmax_ok"))
        v2p_ok, v2_ok, pr_ok, tp_ok, prT_ok = (sem(n) for n in ("v2p_ok", "v2_ok", "pr_ok", "tp_ok", "prT_ok"))
        pv_ok, rps_ok, pvm_ok, sel_ok, ao_ok = (sem(n) for n in ("pv_ok", "rps_ok", "pvm_ok", "sel_ok", "ao_ok"))
        xcbo_ok = sem("xcbo_ok")
        passed, dve_carry, sp_carry = sem("passed"), sem("dve_carry"), sem("sp_carry")
        mid_pe, mid_dve, mid_pool = sem("mid_pe"), sem("mid_dve"), sem("mid_pool")
        xh_ok, xhT_ok, hg_ok, hT_ok = sem("xh_ok"), sem("xhT_ok"), sem("hg_ok"), sem("hT_ok")
        up_ok, th_ok, sg_ok, act_ok = (sem(n) for n in ("up_ok", "th_ok", "sg_ok", "act_ok"))
        ta_ok, actT_ok, y_ok, o2s_ok, to_ok = (sem(n) for n in ("ta_ok", "actT_ok", "y_ok", "o2s_ok", "to_ok"))
        o2_ok, kvp_ok, kT_ok, vT_ok = (sem(n) for n in ("o2_ok", "kvp_ok", "kT_ok", "vT_ok"))
        saved = [sem("saved0"), sem("saved1")]
        xs_in = [sem("xs_in0"), sem("xs_in1")]
        stored = [sem("stored0"), sem("stored1")]
        bdk_ok, bdv_ok, ap_ok, a_ok = (sem(n) for n in ("bdk_ok", "bdv_ok", "ap_ok", "a_ok"))
        vwp_ok, vw_ok = sem("vwp_ok"), sem("vw_ok")
        sp_ok, mx_ok, sx_ok, ep_ok = (sem(n) for n in ("sp_ok", "mx_ok", "sx_ok", "ep_ok"))
        sm_ok, rsm_ok, at_ok, tt_ok, atT_ok = (sem(n) for n in ("sm_ok", "rsm_ok", "at_ok", "tt_ok", "atT_ok"))
        op_ok, ob_ok = sem("op_ok"), sem("ob_ok")

        x_rows = x.rearrange("b (p j) d -> p b (j d)", j=2)
        out_rows = out.rearrange("b (p j) d -> p b (j d)", j=2)

        def over(ap, n):
            return ap.unsqueeze(2).broadcast_to([ap.shape[0], ap.shape[1], n])

        def under(ap, n):
            return ap.unsqueeze(1).broadcast_to([ap.shape[0], n, ap.shape[1]])

        def heads(ap, n):
            return ap.rearrange("p (m n) -> p m n", n=n)

        block = ctx.enter_context(nc.Block())

        N_ATTN, N_SLOTS, N_REST = 8, 17, 4

        @block.sync
        def _(sp):
            def load(done, *pairs):
                for to, what in pairs:
                    sp.dma_start(to, what).then_inc(done, 16)

            def row(r, v):
                return vec[r:r + 1, :], v.rearrange("(o d) -> o d", o=1)

            load(w_attn, (W[:, AQ, :], a_Wq), (W[:, AK, :], a_Wk), row(BQ, a_bq), row(BK, a_bk), row(BV, a_bv),
                 (Rrep[:, :], R.unsqueeze(0).broadcast_to([H, DH, DH])), (W[:, AV, :], a_Wv), (W[:, AO, :], a_Wo))
            load(w_slots, (a_bo_all[:, :], a_bo.partition_broadcast(P)), (W[:, DK, :], d_Wk),
                 (W[:, DV, :], d_Wv), (W[:, CQ, :], c_Wq), (W[:, DQ, :], d_Wq),
                 (vec[SLOT:SLOT + S, :], slot.rearrange("o s d -> (o s) d")), (vec[GAIN:GAIN + S, :], ln_g),
                 (vec[SHIFT:SHIFT + S, :], ln_b), (vec[B2:B2 + S, :], b2), row(BDK, d_bk), row(BDV, d_bv),
                 row(BCQ, c_bq), row(BDQ, d_bq), row(BCK, c_bk), row(BCV, c_bv),
                 (d_bo_all[:, :], d_bo.partition_broadcast(S)), (c_bo_all[:, :], c_bo.partition_broadcast(P)))
            for g in range(1, 4):
                sp.dma_start(X[:, 4 * g:4 * g + 4, :], x_rows[:, 4 * g:4 * g + 4, :]).then_inc(x_in[g], 16)
            load(w_rest, (W[:, DO, :], d_Wo), (W[:, CK, :], c_Wk), (W[:, CV, :], c_Wv), (W[:, CO, :], c_Wo))

            def load_hidden_bias():
                sp.wait_ge(su_act, 2)
                load(f_in, *((fvec[k * Q:k * Q + S, u * F:(u + 1) * F], v) for k in range(3)
                             for u, v in enumerate((b1, bg))))

            def load_experts(g):
                sp.dma_start(W1s[:, g:g + 4, :], W1[g:g + 4].rearrange("e d f -> d e f")).then_inc(e_in, 16)
                sp.dma_start(Wgs[:, g:g + 4, :], Wg[g:g + 4].rearrange("e d f -> d e f")).then_inc(e_in, 16)
                for e in range(g, g + 4):
                    sp.dma_start(W2s[:, e], W2[e].rearrange("(c f) d -> f c d", f=P)).then_inc(e_in, 16)

            def first_loads():
                load_hidden_bias()
                load_experts(4)

            def save(half, par):
                if live(half, par, 4):
                    b, k, n = turn(half, par, 4)
                    wait(sp, xn2T_ok, b + 1)
                    sp.sem_inc(sp_carry, 1)
                    sp.dma_start(XN2T[:, b, :], xn2T[:, k, :]).then_inc(saved[k], 16)
            pipeline(sp, save, NB + LAGS1, FIRST1, NB,
                     {0: lambda: load_experts(0), 4: first_loads, 6: lambda: load_experts(8),
                      8: lambda: load_experts(12)})
            for k in range(2):
                sp.wait_ge(saved[k], 16 * NB // 2)
            sp.wait_ge(s_ok, NB)
            sp.wait_ge(v2p_ok, NB)

            def move(half, par):
                if live(half, par, 0):
                    b, k, n = turn(half, par, 0)
                    wait(sp, sp_ok, b - 1)
                    sp.sem_inc(sp_carry, 1)
                    sp.dma_start(xs[:, k, :], XN2T[:, b, :]).then_inc(xs_in[k], 16)
                if live(half, par, 7):
                    b, k, n = turn(half, par, 7)
                    wait(sp, ob_ok, b + 1)
                    sp.sem_inc(sp_carry, 1)
                    sp.dma_start(out_rows[:, b, :], ob[:, k, :]).then_inc(stored[k], 16)
            pipeline(sp, move, NB + LAGS2, FIRST2, NB)
            for k in range(2):
                sp.wait_ge(stored[k], 16 * NB // 2)

        @block.gpsimd
        def _(pool):
            made = [0]

            def own(instruction):
                instruction.then_inc(pool_own, 1)
                made[0] += 1
                pool.wait_ge(pool_own, made[0])

            own(pool.memset(ident[:, :], 0.0))
            pool.affine_select(out=ident[:, :], in_=ident[:, :], compare_op=ALU.not_equal, fill=1.0, base=0,
                               pattern=[[-1, P]], channel_multiplier=1).then_inc(ident_ok, 1)
            pool.memset(epsT[:, :], EPS)
            pool.memset(mhalf[:, :], -0.5)
            pool.memset(xn[:, :, :, :], 1.0).then_inc(ones_ok, 1)
            pool.wait_ge(ones_ok, 1)
            own(pool.memset(head8[:, :], 1.0))
            for sign in (1, -1):
                own(pool.affine_select(out=head8[:, :], in_=head8[:, :], compare_op=ALU.is_ge, fill=0.0,
                                       base=0 if sign > 0 else DH - 1, pattern=[[-sign * DH, H]],
                                       channel_multiplier=sign))
            pool.sem_inc(masks_ok, 1)

            def other_masks():
                own(pool.memset(head16[:, :], 1.0))
                for sign in (1, -1):
                    own(pool.affine_select(out=head16[:, :], in_=head16[:, :], compare_op=ALU.is_ge, fill=0.0,
                                           base=0 if sign > 0 else S - 1, pattern=[[-sign * S, P // S]],
                                           channel_multiplier=sign))
                own(pool.memset(sel3[:, :, :], 0.0))
                own(pool.affine_select(out=sel3[:, :, :], in_=sel3[:, :, :], compare_op=ALU.not_equal, fill=1.0,
                                       base=0, pattern=[[-S, P // S], [-1, S]], channel_multiplier=1))
                own(pool.memset(repS[:, :, :], 0.0))
                each = repS[:, :, :].rearrange("p g (j b) -> p (g j) b", b=Q)
                own(pool.affine_select(out=each, in_=each, compare_op=ALU.not_equal, fill=1.0,
                                       base=0, pattern=[[-1, S], [0, Q]], channel_multiplier=1))
                pool.sem_inc(masks_ok, 1)

            def paddings():
                own(pool.memset(aoT[:, :, :], 0.0))
                own(pool.memset(xn2[:, :, :, :], 1.0))
                pool.sem_inc(masks_ok, 1)
                pool.wait_ge(w_slots, 16 * N_SLOTS)

            def experts_masks():
                own(pool.memset(hT[:, :, :], 0.0))
                own(pool.memset(rep3[:, :, :], 0.0))
                each3 = rep3[:, :, :].rearrange("p g (j b) -> p (g j) b", b=Q)
                for k in range(3):
                    own(pool.affine_select(out=each3, in_=each3, compare_op=ALU.not_equal, fill=1.0,
                                           base=-k * Q, pattern=[[-1, S], [0, Q]], channel_multiplier=1))
                pool.sem_inc(masks_ok, 1)

            def rest_of_parts(n, u):
                pool.wait_ge(parts_act, n + 1)
                half = slice(u * F, (u + 1) * F)
                pool.tensor_tensor(fvec[:, half], fvec[:, half], parts[:, n, half],
                                   ALU.subtract).then_inc(parts_pool, 1)

            def step(half, par):
                if live(half, par, 0):
                    b, k, n = turn(half, par, 0)
                    wait(pool, mv1_ok, b + 1)
                    pool.tensor_tensor(ve1[:, k, :], mv1[:, k, :, 1], epsT[:, 0:2], ALU.add).then_inc(ve1_ok, 1)
                    wait(pool, ve1_ok, b + 1)
                    pool.tensor_tensor(rs1[:, k, :], ve1[:, k, :], mhalf[:, 0:2], ALU.pow).then_inc(rs1_ok, 1)
                if live(half, par, 2):
                    b, k, n = turn(half, par, 2)
                    wait(pool, xn_ok, b + 1)
                    pool.tensor_tensor(X[:, b, :].rearrange("p (j d) -> p j d", j=2),
                                       X[:, b, :].rearrange("p (j d) -> p j d", j=2),
                                       under(a_bo_all[:, :], 2), ALU.add).then_inc(xbo_ok, 1)
                if live(half, par, 3):
                    b, k, n = turn(half, par, 3)
                    wait(pool, mv2_ok, b + 1)
                    pool.tensor_tensor(ve2[:, k, :], mv2[:, k, :, 1], epsT[:, 0:2], ALU.add).then_inc(ve2_ok, 1)
                    wait(pool, ve2_ok, b + 1)
                    pool.tensor_tensor(rs2[:, k, :], ve2[:, k, :], mhalf[:, 0:2], ALU.pow).then_inc(rs2_ok, 1)
                if live(half, par, 2):
                    b, k, n = turn(half, par, 2)
                    wait(pool, rz_ok, b + 1)
                    wait(pool, ft_ok, b + 1)
                    wait(pool, tq_ok, b - 1)
                    for j in range(2):
                        last = pool.tensor_tensor(heads(qz[:, k, j, :], DH), heads(ft[:, k, j, 0:P], DH),
                                                  over(rz[:, k, j * H:(j + 1) * H], DH), ALU.mult)
                    last.then_inc(qz_ok, 1)
                if live(half, par, 5):
                    b, k, n = turn(half, par, 5)
                    wait(pool, xn2_ok, b + 1)
                    pool.tensor_tensor(X[:, b, :].rearrange("p (j d) -> p j d", j=2),
                                       X[:, b, :].rearrange("p (j d) -> p j d", j=2),
                                       under(c_bo_all[:, :], 2), ALU.add).then_inc(xcbo_ok, 1)

            pipeline(pool, step, NB + LAGS1, FIRST1, NB,
                     {1: other_masks, 2: paddings, 6: lambda: rest_of_parts(0, 0), 7: lambda: rest_of_parts(0, 1),
                      NB + 1: lambda: rest_of_parts(1, 0), NB + 2: lambda: rest_of_parts(1, 1)})
            experts_masks()

            pool.wait_ge(mid_dve, 1 + G)
            pool.tensor_tensor(ve3[:, :], mv3[:, :, 1], epsT[:, :], ALU.add).then_inc(mid_pool, 1)
            pool.wait_ge(mid_pool, 1)
            pool.tensor_tensor(rs3[:, :], ve3[:, :], mhalf[:, :], ALU.pow).then_inc(mid_pool, 1)

            def step2(half, par):
                if live(half, par, 5):
                    b, k, n = turn(half, par, 5)
                    wait(pool, vwp_ok, b - 1)
                    pool.tensor_tensor(heads(BDv[:, k, :], S), under(vT[:, :, b], H), over(head8[:, :], S),
                                       ALU.mult).then_inc(bdv_ok, 1)
                if live(half, par, 1):
                    b, k, n = turn(half, par, 1)
                    wait(pool, ap_ok, b - 1)
                    pool.tensor_tensor(heads(BDk[:, k, :], S), under(kT[:, :, b], H), over(head8[:, :], S),
                                       ALU.mult).then_inc(bdk_ok, 1)
                if live(half, par, 6):
                    b, k, n = turn(half, par, 6)
                    wait(pool, rsm_ok, b + 1)
                    wait(pool, tt_ok, b - 1)
                    for j in range(2):
                        last = pool.tensor_tensor(heads(at[:, k, j * HS:(j + 1) * HS], S),
                                                  heads(ep[:, k, j * HS:(j + 1) * HS], S),
                                                  over(rsm[:, k, j * H:(j + 1) * H], S), ALU.mult)
                    last.then_inc(at_ok, 1)

            pool.wait_ge(kT_ok, 1)
            pipeline(pool, step2, NB + LAGS2, FIRST2, NB, {1: lambda: pool.wait_ge(vT_ok, 1)})

        @block.scalar
        def _(sc):
            sc.dma_start(X[:, 0:4, :], x_rows[:, 0:4, :]).then_inc(x_in[0], 16)

            def attention_weights():
                sc.wait_ge(su_pe, 2)
                sc.activation(Wproj[:, 0:2 * P], ps[:, 4, 0:2 * P], ACT.Copy, scale=0.25)
                sc.activation(WvP[:, :], ps[:, 4, 2 * P:3 * P], ACT.Copy)
                sc.activation(WoT[:, :], ps[:, 4, 3 * P:4 * P], ACT.Copy)
                sc.wait_ge(su_pe, 3)
                sc.activation(Wproj[:, 2 * P:4 * P], ps[:, 5, 0:2 * P], ACT.Copy, scale=SC).then_inc(su_act, 1)

            def slot_weights():
                sc.wait_ge(su_pe, 6)
                sc.activation(dWvP[:, :], ps[:, 7, 2 * P:3 * P], ACT.Copy)
                sc.activation(Ad[:, :], ps[:, 4, 0:HS], ACT.Copy).then_inc(su_act, 1)

            def part0():
                sc.wait_ge(f_in, 16 * 6)
                sc.activation(parts[:, 0, :], fvec, ACT.Copy).then_inc(parts_act, 1)

            def part1_all():
                sc.wait_ge(parts_pool, 2)
                sc.activation(parts[:, 1, :], fvec, ACT.Copy)

            def part1():
                sc.activation(parts[Q:2 * Q, 0, :], fvec[Q:2 * Q], ACT.Copy).then_inc(parts_act, 1)

            def part2():
                sc.wait_ge(parts_pool, 4)
                sc.activation(parts[2 * Q:, 0, :], fvec[2 * Q:], ACT.Copy).then_inc(parts_act, 1)

            def step(half, par):
                if live(half, par, 4):
                    b, k, n = turn(half, par, 4)
                    wait(sc, tx2_ok, b + 1)
                    wait(sc, v2p_ok, b - 1)
                    wait(sc, saved[k], n * 16, NB * 8)
                    sc.activation(xn2T[:, k, :], ps[:, 3, 0:NT], ACT.Copy).then_inc(xn2T_ok, 1)
                if live(half, par, 2):
                    b, k, n = turn(half, par, 2)
                    wait(sc, vp_ok, b + 1)
                    wait(sc, kv_ok, b - 1)
                    sc.activation(Vs[:, k], ps[:, 2, 0:2 * P].rearrange("p (j d) -> p j d", j=2),
                                  ACT.Copy).then_inc(v_ok, 1)
                if live(half, par, 3):
                    b, k, n = turn(half, par, 3)
                    wait(sc, tq_ok, b + 1)
                    wait(sc, out_ok, b - 1)
                    sc.activation(qzT[:, k, :], ps[:, 5, 0:NT], ACT.Copy).then_inc(qzT_ok, 1)
                if live(half, par, 3):
                    b, k, n = turn(half, par, 3)
                    wait(sc, tq_ok, b + 1)
                    wait(sc, out_ok, b - 1)
                    sc.activation(Mb[:, k, :], ps[:, 5, NT:NT + P], ACT.Copy).then_inc(mb_ok, 1)
                if live(half, par, 1):
                    b, k, n = turn(half, par, 1)
                    wait(sc, tx_ok, b + 1)
                    wait(sc, vp_ok, b - 1)
                    sc.activation(xnT[:, k, :], ps[:, 3, 0:NT], ACT.Copy).then_inc(xnT_ok, 1)
                if live(half, par, 2):
                    b, k, n = turn(half, par, 2)
                    wait(sc, ex_ok, b + 1)
                    wait(sc, kv_ok, b - 1)
                    wait(sc, qz_ok, b - 1)
                    sc.activation(ft[:, k], ex[:, k], ACT.Exp).then_inc(ft_ok, 1)
                if live(half, par, 4):
                    b, k, n = turn(half, par, 4)
                    wait(sc, v2p_ok, b + 1)
                    wait(sc, pv_ok, b - 1)
                    sc.activation(V2s[:, k], ps[:, 2, 0:2 * P].rearrange("p (j d) -> p j d", j=2),
                                  ACT.Copy).then_inc(v2_ok, 1)
                if live(half, par, 4):
                    b, k, n = turn(half, par, 4)
                    wait(sc, nmax_ok, b + 1)
                    wait(sc, tp_ok, b - 1)
                    wait(sc, rps_ok, b - 1)
                    for hf in range(2):
                        last = sc.activation(pr[:, k, hf, :], ps[:, 4, hf * NT:(hf + 1) * NT], ACT.Exp,
                                             bias=nmax[:, k, hf:hf + 1], accum_out=psm[:, k, hf:hf + 1])
                    last.then_inc(pr_ok, 1)
                if live(half, par, 1):
                    b, k, n = turn(half, par, 1)
                    wait(sc, proj_ok, b + 1)
                    wait(sc, ss_ok, b - 1)
                    sc.activation(sq[:, k], ps[:, 0:2, 0:2 * P], ACT.Square).then_inc(sq_ok, 1)
                if live(half, par, 4):
                    b, k, n = turn(half, par, 4)
                    wait(sc, tp_ok, b + 1)
                    wait(sc, pv_ok, b - 1)
                    sc.activation(prT[:, k], ps[:, 5, :].rearrange("p (j m) -> p j m", j=2),
                                  ACT.Copy).then_inc(prT_ok, 1)

            pipeline(sc, step, NB + LAGS1, FIRST1, NB,
                     {1: attention_weights, 3: slot_weights,
                      5: part0, 8: part1_all, NB: part1, NB + 3: part2})

            def act_columns(g):
                sc.wait_ge(ta_ok, g + 1)
                if g >= 2:
                    sc.wait_ge(y_ok, g - 1)
                sc.activation(actT[:, g % 2], ps[:, 1, :].rearrange("p (c m) -> p c m", c=FC),
                              ACT.Copy).then_inc(actT_ok, 1)

            for g in range(G):
                bank = 2 + 2 * (g % 3)
                if g >= 2:
                    sc.wait_ge(sg_ok, g - 1)
                for u in range(2):
                    sc.wait_ge(up_ok, 2 * g + u + 1)
                    sc.activation(th[g % 2][:, u, :], ps[:, bank + u, :], ACT.Tanh, scale=0.5).then_inc(th_ok, 1)
                if g >= 1:
                    act_columns(g - 1)
            act_columns(G - 1)

            def step2(half, par):
                if live(half, par, 3):
                    b, k, n = turn(half, par, 3)
                    wait(sc, sx_ok, b + 1)
                    wait(sc, at_ok, b - 1)
                    wait(sc, sm_ok, b - 1)
                    sc.activation(ep[:, k, :], sx[:, k, :], ACT.Exp).then_inc(ep_ok, 1)
                if live(half, par, 0):
                    b, k, n = turn(half, par, 0)
                    wait(sc, ap_ok, b + 1)
                    wait(sc, sp_ok, b - 1)
                    sc.activation(As[:, k, :], ps[:, k, 0:HS], ACT.Copy).then_inc(a_ok, 1)
                if live(half, par, 5):
                    b, k, n = turn(half, par, 5)
                    wait(sc, tt_ok, b + 1)
                    wait(sc, op_ok, b - 1)
                    sc.activation(atT[:, k], ps[:, 4 + k, :].rearrange("p (h t) -> p h t", h=2),
                                  ACT.Copy).then_inc(atT_ok, 1)
                if live(half, par, 4):
                    b, k, n = turn(half, par, 4)
                    wait(sc, vwp_ok, b + 1)
                    wait(sc, op_ok, b - 1)
                    sc.activation(VWs[:, k, :], ps[:, 1 - k, 0:HS], ACT.Copy).then_inc(vw_ok, 1)

            pipeline(sc, step2, NB + LAGS2, FIRST2, NB)

        @block.vector
        def _(ve):
            def attention_weights():
                ve.wait_ge(w_attn, 16 * N_ATTN)
                for m in (AQ, AK, AV):
                    ve.tensor_scalar(W[:, m, 0:L], W[:, m, 0:L], W[:, m, L:P], None, ALU.subtract)
                ve.wait_ge(su_pe, 1)
                ve.tensor_copy(vecT[:, BQ:BV + 1], ps[:, 7, 0:BV + 1 - BQ]).then_inc(passed, 1)
                ve.wait_ge(passed, 1)
                ve.tensor_copy(W[:, AQ:AV + 1, L], vecT[:, BQ:BV + 1]).then_inc(su_dve, 1)
                ve.wait_ge(masks_ok, 1)
                ve.tensor_tensor(heads(BDR[:, :], DH), under(Rrep[:, :], H), over(head8[:, :], DH),
                                 ALU.mult).then_inc(su_dve, 1)

            def slot_weights():
                ve.wait_ge(masks_ok, 3)
                ve.tensor_reduce(selS[:, :], sel3[:, :, :].rearrange("p h s -> p s h"), AX.X, ALU.add)
                ve.wait_ge(w_slots, 16 * N_SLOTS)
                ve.tensor_tensor(slotb[:, :], vec[SLOT:SLOT + S, :], d_bo_all[:, :], ALU.add)
                ve.wait_ge(su_pe, 4)
                ve.tensor_copy(vecT[:, :], ps[:, 7, 0:NR]).then_inc(su_dve, 1)
                for m in range(3):
                    last = ve.tensor_scalar(Wt[:, m, 0:L], ps[:, 4, m * P:m * P + L],
                                            ps[:, 4, m * P + L:(m + 1) * P], None, ALU.subtract)
                last.then_inc(passed, 1)
                ve.wait_ge(passed, 2)
                ve.tensor_copy(Wt[:, :, L], vecT[:, BDK:BCQ + 1])
                ve.wait_ge(su_pe, 5)
                ve.tensor_scalar(qTs[:, :], ps[:, 7, P:P + S], vecT[:, BDQ:BDQ + 1], SC, ALU.add,
                                 ALU.mult).then_inc(passed, 1)
                ve.wait_ge(passed, 3)
                ve.tensor_tensor(heads(qbd[:, :], S), under(qTs[:, :], H), over(head8[:, :], S),
                                 ALU.mult).then_inc(su_dve, 1)

            def later_x():
                for g in (2, 3):
                    ve.wait_ge(x_in[g], 16)

            def step(half, par):
                if live(half, par, 3):
                    b, k, n = turn(half, par, 3)
                    wait(ve, den2_ok, b + 1)
                    wait(ve, qz_ok, b - 1)
                    ve.reciprocal(rz[:, k, :], den2[:, k, :]).then_inc(rz_ok, 1)
                if live(half, par, 4):
                    b, k, n = turn(half, par, 4)
                    wait(ve, rs2_ok, b + 1)
                    wait(ve, tx2_ok, b - 1)
                    for j in range(2):
                        last = ve.tensor_scalar(xn2[:, k, j, 0:L], X[:, b, j * P:j * P + L], mv2[:, k, j, 0:1],
                                                rs2[:, k, j:j + 1], ALU.subtract, ALU.mult)
                    last.then_inc(xn2_ok, 1)
                if live(half, par, 1):
                    b, k, n = turn(half, par, 1)
                    wait(ve, rs1_ok, b + 1)
                    wait(ve, tx_ok, b - 1)
                    for j in range(2):
                        last = ve.tensor_scalar(xn[:, k, j, 0:L], X[:, b, j * P:j * P + L], mv1[:, k, j, 0:1],
                                                rs1[:, k, j:j + 1], ALU.subtract, ALU.mult)
                    last.then_inc(xn_ok, 1)
                if live(half, par, 3):
                    b, k, n = turn(half, par, 3)
                    wait(ve, kv_ok, b + 1)
                    wait(ve, tq_ok, b - 1)
                    ve.tensor_tensor(heads(kvm[:, k, :], DH), heads(ps[:, 6, NT:NT + P], DH), over(head8[:, :], DH),
                                     ALU.mult).then_inc(kvm_ok, 1)
                if live(half, par, 0):
                    b, k, n = turn(half, par, 0)
                    for j in range(2):
                        last = ve.bn_stats(st1[:, k, j, :], X[:, b, j * P:(j + 1) * P])
                    last.then_inc(bn1_ok, 1)
                if live(half, par, 6):
                    b, k, n = turn(half, par, 6)
                    wait(ve, sel_ok, b + 1)
                    ve.tensor_scalar(aoT[:, :, b], ps[:, 7, P:P + S], 1.0, None,
                                     ALU.mult).then_inc(ao_ok, 1)
                if live(half, par, 2):
                    b, k, n = turn(half, par, 2)
                    wait(ve, sq_ok, b + 1)
                    ve.tensor_reduce(ss[:, k, :].rearrange("p (j h) -> p j h", j=2),
                                     sq[:, k].rearrange("p j (h d) -> p j h d", d=DH), AX.X,
                                     ALU.add).then_inc(ss_ok, 1)
                if live(half, par, 0):
                    b, k, n = turn(half, par, 0)
                    wait(ve, bn1_ok, b + 1)
                    wait(ve, rs1_ok, b - 1)
                    ve.sem_inc(dve_carry, 1)
                    for j in range(2):
                        last = ve.bn_aggr(mv1[:, k, j, :], st1[:, k, j, :])
                    last.then_inc(mv1_ok, 1)
                if live(half, par, 2):
                    b, k, n = turn(half, par, 2)
                    wait(ve, ss_ok, b + 1)
                    wait(ve, ft_ok, b - 1)
                    ve.tensor_tensor(ex[:, k].rearrange("p j (h d) -> p j h d", d=DH),
                                     ps[:, 0:2, 2 * P:4 * P].rearrange("p j (h d) -> p j h d", d=DH),
                                     ss[:, k, :].rearrange("p (j h) -> p j h", j=2).unsqueeze(3)
                                     .broadcast_to([P, 2, 2 * H, DH]), ALU.subtract).then_inc(ex_ok, 1)
                if live(half, par, 4):
                    b, k, n = turn(half, par, 4)
                    wait(ve, s_ok, b + 1)
                    ve.tensor_reduce(nmax[:, k, :], ps[:, 4, :].rearrange("p (h t) -> p h t", h=2), AX.X,
                                     ALU.max, negate=True).then_inc(nmax_ok, 1)
                if live(half, par, 3):
                    b, k, n = turn(half, par, 3)
                    wait(ve, out_ok, b + 1)
                    wait(ve, xbo_ok, b + 1)
                    ve.tensor_tensor(X[:, b, :], ps[:, 6, 0:NT], X[:, b, :], ALU.add).then_inc(x2_ok, 1)
                if live(half, par, 3):
                    b, k, n = turn(half, par, 3)
                    wait(ve, x2_ok, b + 1)
                    ve.sem_inc(dve_carry, 1)
                    for j in range(2):
                        last = ve.bn_stats(st2[:, k, j, :], X[:, b, j * P:(j + 1) * P])
                    last.then_inc(bn2_ok, 1)
                if live(half, par, 5):
                    b, k, n = turn(half, par, 5)
                    wait(ve, pr_ok, b + 1)
                    ve.reciprocal(rps[:, k, :], psm[:, k, :]).then_inc(rps_ok, 1)
                if live(half, par, 3):
                    b, k, n = turn(half, par, 3)
                    wait(ve, bn2_ok, b + 1)
                    ve.sem_inc(dve_carry, 1)
                    for j in range(2):
                        last = ve.bn_aggr(mv2[:, k, j, :], st2[:, k, j, :])
                    last.then_inc(mv2_ok, 1)
                if live(half, par, 2):
                    b, k, n = turn(half, par, 2)
                    wait(ve, ft_ok, b + 1)
                    ve.tensor_reduce(den[:, k, :].rearrange("p (j h) -> p j h", j=2),
                                     ft[:, k, :, 0:P].rearrange("p j (h d) -> p j h d", d=DH), AX.X,
                                     ALU.add).then_inc(den_ok, 1)
                if live(half, par, 2):
                    b, k, n = turn(half, par, 2)
                    wait(ve, den_ok, b + 1)
                    ve.tensor_scalar(den2[:, k, :], den[:, k, :], 1e-8, None, ALU.add).then_inc(den2_ok, 1)
                if live(half, par, 5):
                    b, k, n = turn(half, par, 5)
                    wait(ve, rps_ok, b + 1)
                    wait(ve, pv_ok, b + 1)
                    wait(ve, sel_ok, b - 1)
                    for hf in range(2):
                        last = ve.scalar_tensor_tensor(
                            out=heads(pvm[:, k, hf * 64:hf * 64 + 64], DH),
                            in0=heads(ps[:, 7, hf * 64:hf * 64 + 64], DH),
                            scalar=rps[:, k, hf:hf + 1], in1=over(head16[:, :], DH), op0=ALU.mult, op1=ALU.mult)
                    last.then_inc(pvm_ok, 1)

            ve.wait_ge(x_in[0], 16)
            ve.wait_ge(ones_ok, 1)
            pipeline(ve, step, NB + LAGS1, FIRST1, NB,
                     {1: attention_weights, 3: slot_weights, 4: lambda: ve.wait_ge(x_in[1], 16), 8: later_x})

            ve.wait_ge(mid_pe, 1)
            for g in range(G):
                last = ve.bn_stats(st3[:, g, :], ps[:, 0, g * P:(g + 1) * P])
            last.then_inc(mid_dve, 1)
            ve.wait_ge(mid_dve, 1)
            for g in range(G):
                ve.bn_aggr(mv3[:, g, :], st3[:, g, :]).then_inc(mid_dve, 1)
            ve.wait_ge(mid_pool, 2)
            for half in range(2):
                for g in (2 * half, 2 * half + 1):
                    last = ve.tensor_scalar(xh[:, g, :], ps[:, 0, g * P:(g + 1) * P], mv3[:, g, 0:1],
                                            rs3[:, g:g + 1], ALU.subtract, ALU.mult)
                last.then_inc(xh_ok, 1)
            for half in range(2):
                slots = slice(half * S // 2, (half + 1) * S // 2)
                ve.wait_ge(xhT_ok, half + 1)
                ve.tensor_tensor(hg[:, slots, :], ps[:, 1 + 6 * half, 0:2 * P]
                                 .rearrange("p (s b) -> p s b", b=Q)[:, :, 0:NB],
                                 over(vecT[:, GAIN + slots.start:GAIN + slots.stop], NB), ALU.mult).then_inc(hg_ok, 1)
                ve.wait_ge(hg_ok, half + 1)
                ve.tensor_tensor(hT[:, slots, 0:NB], hg[:, slots, :],
                                 over(vecT[:, SHIFT + slots.start:SHIFT + slots.stop], NB),
                                 ALU.add).then_inc(hT_ok, 1)

            for g in range(G):
                bank = 2 + 2 * (g % 3)
                for u in range(2):
                    ve.wait_ge(th_ok, 2 * g + u + 1)
                    last = ve.scalar_tensor_tensor(out=sg[g % 2][:, u, :], in0=th[g % 2][:, u, :], scalar=1.0,
                                                   in1=ps[:, bank + u, :], op0=ALU.add, op1=ALU.mult)
                last.then_inc(sg_ok, 1)
                ve.wait_ge(sg_ok, g + 1)
                if g >= 2:
                    ve.wait_ge(ta_ok, g - 1)
                ve.scalar_tensor_tensor(out=act[:, g % 2], in0=sg[g % 2][:, 0, :], scalar=0.25,
                                        in1=sg[g % 2][:, 1, :], op0=ALU.mult, op1=ALU.mult).then_inc(act_ok, 1)
            ve.wait_ge(y_ok, G)
            ve.tensor_copy(o2[:, :, :], ps[:, 0, :].rearrange("p (g d) -> p g d", g=G)).then_inc(o2s_ok, 1)
            ve.wait_ge(to_ok, 1)
            ve.tensor_tensor(o2T[:, :].rearrange("p (s b) -> p s b", b=NB),
                             ps[:, 1, :].rearrange("p (s b) -> p s b", b=Q)[:, :, 0:NB],
                             over(vecT[:, B2:B2 + S], NB), ALU.add).then_inc(o2_ok, 1)
            ve.wait_ge(kvp_ok, 1)
            ve.tensor_scalar(kT[:, :, :].rearrange("p s b -> p (s b)"), ps[:, 6, 0:2 * P],
                             vecT[:, BCK:BCK + 1], SC, ALU.add, ALU.mult).then_inc(kT_ok, 1)
            ve.wait_ge(kvp_ok, 2)
            ve.tensor_scalar(vT[:, :, :].rearrange("p s b -> p (s b)"), ps[:, 7, 0:2 * P],
                             vecT[:, BCV:BCV + 1], None, ALU.add).then_inc(vT_ok, 1)

            def step2(half, par):
                if live(half, par, 1):
                    b, k, n = turn(half, par, 1)
                    wait(ve, mx_ok, b + 1)
                    wait(ve, ep_ok, b - 1)
                    ve.tensor_tensor(heads(sx[:, k, :], S), heads(ps[:, 2 + k, :], S), over(mx[:, k, :], S),
                                     ALU.subtract).then_inc(sx_ok, 1)
                if live(half, par, 2):
                    b, k, n = turn(half, par, 2)
                    wait(ve, ep_ok, b + 1)
                    ve.tensor_reduce(sm[:, k, :], heads(ep[:, k, :], S), AX.X, ALU.add).then_inc(sm_ok, 1)
                if live(half, par, 2):
                    b, k, n = turn(half, par, 2)
                    wait(ve, sm_ok, b + 1)
                    wait(ve, at_ok, b - 1)
                    ve.reciprocal(rsm[:, k, :], sm[:, k, :]).then_inc(rsm_ok, 1)
                if live(half, par, 5):
                    b, k, n = turn(half, par, 5)
                    wait(ve, op_ok, b + 1)
                    wait(ve, stored[k], n * 16, NB * 8)
                    ve.tensor_tensor(ob[:, k, :], ps[:, 6 + k, 0:NT], X[:, b, :], ALU.add).then_inc(ob_ok, 1)
                if live(half, par, 0):
                    b, k, n = turn(half, par, 0)
                    wait(ve, sp_ok, b + 1)
                    ve.tensor_reduce(mx[:, k, :], heads(ps[:, 2 + k, :], S), AX.X, ALU.max).then_inc(mx_ok, 1)

            ve.wait_ge(xcbo_ok, NB)
            pipeline(ve, step2, NB + LAGS2, FIRST2, NB)

        @block.tensor
        def _(pe):
            def attention_weights():
                pe.wait_ge(ident_ok, 1)
                pe.wait_ge(w_attn, 16 * N_ATTN)
                pe.transpose(ps[:, 7, 0:BV + 1 - BQ], vec[BQ:BV + 1, :],
                             ident[BQ:BV + 1, BQ:BV + 1]).then_inc(su_pe, 1)
                pe.wait_ge(su_dve, 1)
                for n, m in enumerate((AQ, AK, AV, AO)):
                    last = pe.transpose(ps[:, 4, n * P:(n + 1) * P], W[:, m, :], ident[:, :])
                last.then_inc(su_pe, 1)
                pe.wait_ge(su_dve, 2)
                for n, m in enumerate((AQ, AK)):
                    last = pe.matmul(ps[:, 5, n * P:(n + 1) * P], W[:, m, :], BDR[:, :], start=True, stop=True)
                last.then_inc(su_pe, 1)
                pe.wait_ge(su_act, 1)

            def slot_weights():
                pe.wait_ge(w_slots, 16 * N_SLOTS)
                pe.transpose(ps[:, 7, 0:NR], vec[:, :], ident[0:NR, 0:NR])
                for n, m in enumerate((DK, DV, CQ)):
                    last = pe.transpose(ps[:, 4, n * P:(n + 1) * P], W[:, m, :], ident[:, :])
                last.then_inc(su_pe, 1)
                pe.wait_ge(su_dve, 3)
                pe.matmul(ps[:, 7, P:P + S], W[:, DQ, :], vecT[:, SLOT:SLOT + S], start=True,
                          stop=True).then_inc(su_pe, 1)
                pe.wait_ge(su_dve, 4)
                pe.transpose(ps[:, 7, 2 * P:3 * P], Wt[:, 1, :], ident[:, :])
                pe.matmul(ps[:, 4, 0:HS], Wt[:, 0, :], qbd[:, :], start=True, stop=True).then_inc(su_pe, 1)

            def slots_start():
                for g in range(G):
                    pe.matmul(ps[:, 0, g * P:(g + 1) * P], repS[:, g, :], slotb[:, :], start=(g == 0), stop=False,
                              skip_group_check=True)

            def step(half, par):
                if live(half, par, 2):
                    b, k, n = turn(half, par, 2)
                    wait(pe, xnT_ok, b + 1)
                    wait(pe, ex_ok, b)
                    for j in range(2):
                        last = pe.matmul(ps[:, j, :], xnT[:, k, j * P:(j + 1) * P], Wproj[:, :], start=True,
                                         stop=True)
                    last.then_inc(proj_ok, 1)
                if live(half, par, 5):
                    b, k, n = turn(half, par, 5)
                    wait(pe, pr_ok, b + 1)
                    wait(pe, mb_ok, b + 2)
                    for j in range(2):
                        for hf in range(2):
                            last = pe.transpose(ps[:, 5, j * HS + hf * P:j * HS + (hf + 1) * P],
                                                pr[:, k, hf, j * P:(j + 1) * P], ident[:, :])
                    last.then_inc(tp_ok, 1)
                if live(half, par, 3):
                    b, k, n = turn(half, par, 3)
                    wait(pe, ft_ok, b + 1)
                    wait(pe, v_ok, b + 1)
                    wait(pe, x2_ok, b)
                    for j in range(2):
                        last = pe.matmul(ps[:, 6, NT:NT + P], Vs[:, k, j, :], ft[:, k, j, P:2 * P], start=(j == 0),
                                         stop=(j == 1))
                    last.then_inc(kv_ok, 1)
                if live(half, par, 4):
                    b, k, n = turn(half, par, 4)
                    wait(pe, xn2_ok, b + 1)
                    wait(pe, xnT_ok, b + 3)
                    for j in range(2):
                        last = pe.transpose(ps[:, 3, j * P:(j + 1) * P], xn2[:, k, j, :], ident[:, :])
                    last.then_inc(tx2_ok, 1)
                if live(half, par, 6):
                    b, k, n = turn(half, par, 6)
                    wait(pe, pvm_ok, b + 1)
                    pe.matmul(ps[:, 7, P:P + S], pvm[:, k, :], selS[:, :], start=True, stop=True).then_inc(sel_ok, 1)
                if live(half, par, 2):
                    b, k, n = turn(half, par, 2)
                    wait(pe, xnT_ok, b + 1)
                    wait(pe, v2_ok, b - 2)
                    for j in range(2):
                        last = pe.matmul(ps[:, 2, j * P:(j + 1) * P], xnT[:, k, j * P:(j + 1) * P], WvP[:, :],
                                         start=True, stop=True)
                    last.then_inc(vp_ok, 1)
                if live(half, par, 3):
                    b, k, n = turn(half, par, 3)
                    wait(pe, qz_ok, b + 1)
                    wait(pe, prT_ok, b - 1)
                    for j in range(2):
                        pe.transpose(ps[:, 5, j * P:(j + 1) * P], qz[:, k, j, :], ident[:, :])
                if live(half, par, 3):
                    b, k, n = turn(half, par, 3)
                    wait(pe, kvm_ok, b + 1)
                    pe.matmul(ps[:, 5, NT:NT + P], kvm[:, k, :], WoT[:, :], start=True,
                              stop=True).then_inc(tq_ok, 1)
                if live(half, par, 4):
                    b, k, n = turn(half, par, 4)
                    wait(pe, xn2T_ok, b + 1)
                    wait(pe, pr_ok, b)
                    for hf in range(2):
                        last = pe.matmul(ps[:, 4, hf * NT:(hf + 1) * NT], Ad[:, hf * P:(hf + 1) * P],
                                         xn2T[:, k, :], start=True, stop=True)
                    last.then_inc(s_ok, 1)
                if live(half, par, 3):
                    b, k, n = turn(half, par, 3)
                    wait(pe, mb_ok, b + 1)
                    wait(pe, qzT_ok, b + 1)
                    wait(pe, kvm_ok, b + 1)
                    for j in range(2):
                        last = pe.matmul(ps[:, 6, j * P:(j + 1) * P], qzT[:, k, j * P:(j + 1) * P], Mb[:, k, :],
                                         start=True, stop=True)
                    last.then_inc(out_ok, 1)
                if live(half, par, 1):
                    b, k, n = turn(half, par, 1)
                    wait(pe, xn_ok, b + 1)
                    wait(pe, xn2T_ok, b - 2)
                    for j in range(2):
                        last = pe.transpose(ps[:, 3, j * P:(j + 1) * P], xn[:, k, j, :], ident[:, :])
                    last.then_inc(tx_ok, 1)
                if live(half, par, 4):
                    b, k, n = turn(half, par, 4)
                    wait(pe, xn2T_ok, b + 1)
                    wait(pe, v_ok, b + 3)
                    for j in range(2):
                        last = pe.matmul(ps[:, 2, j * P:(j + 1) * P], xn2T[:, k, j * P:(j + 1) * P], dWvP[:, :],
                                         start=True, stop=True)
                    last.then_inc(v2p_ok, 1)
                if live(half, par, 5):
                    b, k, n = turn(half, par, 5)
                    wait(pe, prT_ok, b + 1)
                    wait(pe, v2_ok, b + 1)
                    wait(pe, ao_ok, b)
                    for hf in range(2):
                        for j in range(2):
                            last = pe.matmul(ps[:, 7, hf * 64:hf * 64 + 64], prT[:, k, j, hf * P:(hf + 1) * P],
                                             V2s[:, k, j, hf * 64:hf * 64 + 64], start=(j == 0), stop=(j == 1))
                    last.then_inc(pv_ok, 1)

            pipeline(pe, step, NB + LAGS1, FIRST1, NB,
                     {1: attention_weights, 3: slot_weights, NB + 3: slots_start})

            pe.wait_ge(ao_ok, NB)
            pe.wait_ge(w_rest, 16 * N_REST)
            for g in range(G):
                last = pe.matmul(ps[:, 0, g * P:(g + 1) * P],
                                 aoT[:, g * EG:(g + 1) * EG, :].rearrange("p s b -> p (s b)"), W[:, DO, :],
                                 start=False, stop=False, skip_group_check=True)
            last.then_inc(mid_pe, 1)

            def hidden_bias(g):
                for u in range(2):
                    pe.matmul(ps[:, 2 + 2 * (g % 3) + u, :], rep3[:, g, :], parts[:, 0, u * F:(u + 1) * F],
                              start=True, stop=False, skip_group_check=True)

            def experts_in(g):
                for u, w in enumerate((W1s, Wgs)):
                    for j in range(EG):
                        last = pe.matmul(ps[j * Q:(j + 1) * Q, 2 + 2 * (g % 3) + u, :], hT[:, g * EG + j, :],
                                         w[:, g * EG + j, :], start=False, stop=True, skip_group_check=True)
                    last.then_inc(up_ok, 1)

            def turn_act(g):
                pe.wait_ge(act_ok, g + 1)
                if g >= 1:
                    pe.wait_ge(actT_ok, g)
                for c in range(FC):
                    last = pe.transpose(ps[:, 1, c * P:(c + 1) * P], act[:, g % 2, c * P:(c + 1) * P], ident[:, :])
                last.then_inc(ta_ok, 1)

            def experts_out(g):
                pe.wait_ge(actT_ok, g + 1)
                for c in range(FC):
                    for j in range(EG):
                        last = pe.matmul(ps[j * Q:(j + 1) * Q, 0, g * P:(g + 1) * P],
                                         actT[:, g % 2, c, j * Q:(j + 1) * Q], W2s[:, g * EG + j, c, :],
                                         start=False, stop=(c == FC - 1), skip_group_check=True)
                last.then_inc(y_ok, 1)

            pe.wait_ge(parts_act, 3)
            pe.wait_ge(masks_ok, 4)
            hidden_bias(0)
            hidden_bias(1)
            for half in range(2):
                pe.wait_ge(xh_ok, half + 1)
                for g in range(2):
                    last = pe.transpose(ps[:, 1 + 6 * half, g * P:(g + 1) * P], xh[:, 2 * half + g, :], ident[:, :])
                last.then_inc(xhT_ok, 1)
            pe.wait_ge(hT_ok, 1)
            pe.wait_ge(e_in, 16 * (8 + S))
            experts_in(0)
            experts_in(1)
            pe.wait_ge(hT_ok, 2)
            hidden_bias(2)
            turn_act(0)
            experts_in(2)
            experts_out(0)
            hidden_bias(3)
            turn_act(1)
            experts_in(3)
            experts_out(1)
            for g in (2, 3):
                turn_act(g)
                experts_out(g)
            pe.wait_ge(o2s_ok, 1)
            for g in range(G):
                last = pe.transpose(ps[:, 1, g * P:(g + 1) * P], o2[:, g, :], ident[:, :])
            last.then_inc(to_ok, 1)
            pe.wait_ge(o2_ok, 1)
            pe.matmul(ps[:, 6, 0:2 * P], W[:, CK, :], o2T[:, :], start=True, stop=True).then_inc(kvp_ok, 1)
            pe.matmul(ps[:, 7, 0:2 * P], W[:, CV, :], o2T[:, :], start=True, stop=True).then_inc(kvp_ok, 1)

            def step2(half, par):
                if live(half, par, 2):
                    b, k, n = turn(half, par, 2)
                    wait(pe, a_ok, b + 1)
                    wait(pe, xs_in[k], (n + 1) * 16, NB * 8)
                    wait(pe, sx_ok, b - 1)
                    for j in range(2):
                        last = pe.matmul(ps[:, 2 + k, j * HS:(j + 1) * HS], xs[:, k, j * P:(j + 1) * P],
                                         As[:, k, :], start=True, stop=True)
                    last.then_inc(sp_ok, 1)
                if live(half, par, 4):
                    b, k, n = turn(half, par, 4)
                    wait(pe, bdv_ok, b + 1)
                    wait(pe, a_ok, b + 4)
                    wait(pe, vw_ok, b - 1)
                    for hf in range(2):
                        last = pe.matmul(ps[:, 1 - k, hf * P:(hf + 1) * P], BDv[:, k, hf * P:(hf + 1) * P],
                                         W[:, CO, :], start=True, stop=True)
                    last.then_inc(vwp_ok, 1)
                if live(half, par, 0):
                    b, k, n = turn(half, par, 0)
                    wait(pe, bdk_ok, b + 1)
                    wait(pe, a_ok, b - 1)
                    wait(pe, vw_ok, b - 4)
                    pe.matmul(ps[:, k, 0:HS], Wt[:, 2, :], BDk[:, k, :], start=True, stop=True).then_inc(ap_ok, 1)
                if live(half, par, 5):
                    b, k, n = turn(half, par, 5)
                    wait(pe, at_ok, b + 1)
                    wait(pe, atT_ok, b - 1)
                    for j in range(2):
                        for hf in range(2):
                            last = pe.transpose(ps[:, 4 + k, hf * NT + j * P:hf * NT + (j + 1) * P],
                                                at[:, k, j * HS + hf * P:j * HS + (hf + 1) * P], ident[:, :])
                    last.then_inc(tt_ok, 1)
                if live(half, par, 6):
                    b, k, n = turn(half, par, 6)
                    wait(pe, atT_ok, b + 1)
                    wait(pe, vw_ok, b + 1)
                    wait(pe, ob_ok, b - 1)
                    for j in range(2):
                        for hf in range(2):
                            last = pe.matmul(ps[:, 6 + k, j * P:(j + 1) * P], atT[:, k, hf, j * P:(j + 1) * P],
                                             VWs[:, k, hf * P:(hf + 1) * P], start=(hf == 0),
                                             stop=(hf == 1))
                    last.then_inc(op_ok, 1)

            pipeline(pe, step2, NB + LAGS2, FIRST2, NB)


_INS = ['L0_attn_x', 'L0_attn_Wq', 'L0_attn_bq', 'L0_attn_Wk', 'L0_attn_bk', 'L0_attn_Wv', 'L0_attn_bv',
        'L0_attn_Wo', 'L0_attn_bo', 'L0_attn_R', 'L0_ffn_slot_query', 'L0_ffn_d_Wq', 'L0_ffn_d_Wk', 'L0_ffn_d_Wv',
        'L0_ffn_d_Wo', 'L0_ffn_d_bq', 'L0_ffn_d_bk', 'L0_ffn_d_bv', 'L0_ffn_d_bo', 'L0_ffn_c_Wq', 'L0_ffn_c_Wk',
        'L0_ffn_c_Wv', 'L0_ffn_c_Wo', 'L0_ffn_c_bq', 'L0_ffn_c_bk', 'L0_ffn_c_bv', 'L0_ffn_c_bo', 'L0_ffn_e_ln_g',
        'L0_ffn_e_ln_b', 'L0_ffn_e_W1', 'L0_ffn_e_b1', 'L0_ffn_e_Wg', 'L0_ffn_e_bg', 'L0_ffn_e_W2', 'L0_ffn_e_b2']
_OUTS = [((16, 256, 128), 'float32')]


def kernel(**inputs):
    import numpy as _np
    import concourse.bacc as _bacc
    from concourse import mybir as _mybir
    from concourse.bass_utils import run_bass_kernel_spmd as _run

    nc = _bacc.Bacc("TRN2", target_bir_lowering=False, num_devices=1)
    arrays, args = {}, []
    for name in _INS:
        a = _np.ascontiguousarray(inputs[name])
        arrays[f"in_{name}_dram"] = a
        args.append(nc.dram_tensor(f"in_{name}_dram", a.shape, _mybir.dt.from_np(a.dtype), kind="ExternalInput").ap())
    for i, (shape, dtype) in enumerate(_OUTS):
        dt = _mybir.dt.from_np(_np.dtype(dtype))
        args.append(nc.dram_tensor(f"out_{i}_dram", shape, dt, kind="ExternalOutput").ap())
    build(nc, *args)
    r = _run(nc, [arrays], core_ids=[0])
    got = tuple(r.results[0][f"out_{i}_dram"] for i in range(len(_OUTS)))
    return got[0]
```
